# Optimizing a Trainium2 kernel written in Bass

```python
import numpy as np
import jax
import jax.numpy as jnp

def _softmax(x, axis=-1):
    return jax.nn.softmax(x, axis=axis)

def _gelu(x):
    return jax.nn.gelu(x, approximate=True)

def _silu(x):
    return jax.nn.silu(x)

def _sigmoid(x):
    return jax.nn.sigmoid(x)

def _layernorm(x, axis=-1, eps=1e-05):
    m = jnp.mean(x, axis=axis, keepdims=True)
    v = jnp.var(x, axis=axis, keepdims=True)
    return (x - m) / jnp.sqrt(v + eps)

def _scatter_add(tgt, idx, src, axis=0):
    return tgt.at[idx].add(src)

def _segment_sum(src, seg, n):
    return jax.ops.segment_sum(src, seg, n)
kernel_name = 'mk_seq_preln_d1_jaxref_r4_6215c9'

def setup_inputs(seed: int=0):
    np.random.seed(seed)
    _w = jnp.asarray

    def _L0_attn_setup():
        import jax, jax.numpy as jnp
        import numpy as np
        D_MODEL, D_STATE, D_CONV, EXPAND = (256, 16, 4, 2)
        D_INNER = EXPAND * D_MODEL
        BATCH, SEQ = (2, 512)

        def _forward(x, in_proj_w, conv_w, conv_b, dt_w, dt_b, A_log, D, B_w, C_w, out_w):
            xz = x @ in_proj_w.T
            xc, z = jnp.split(xz, 2, axis=-1)
            h = jnp.transpose(xc, (0, 2, 1))
            h = jnp.pad(h, ((0, 0), (0, 0), (D_CONV - 1, 0)))
            h = jax.lax.conv_general_dilated(h, conv_w, (1,), 'VALID', dimension_numbers=('NCH', 'OIH', 'NCH'))
            h = h + conv_b[None, :, None]
            u = jnp.transpose(h, (0, 2, 1))
            dt = jnp.clip(jax.nn.sigmoid(u @ dt_w.T + dt_b), 0.0001, 1.0)
            A = -jnp.exp(A_log)
            Bm = u @ B_w.T
            Cm = u @ C_w.T
            u_t = jnp.transpose(u, (1, 0, 2))
            dt_t = jnp.transpose(dt, (1, 0, 2))
            B_t = jnp.transpose(Bm, (1, 0, 2))
            C_t = jnp.transpose(Cm, (1, 0, 2))

            def step(state, inp):
                ut, dtt, bt, ct = inp
                dA = jnp.exp(jnp.clip(dtt[:, :, None] * A, -5.0, 5.0))
                dB = dtt[:, :, None] * bt[:, None, :] * ut[:, :, None]
                state = dA * state + dB + 1e-06
                y = jnp.sum(state * ct[:, None, :], axis=-1) + D * ut
                return (state, y)
            state0 = jnp.zeros((x.shape[0], D_INNER, D_STATE), x.dtype)
            _, ys = jax.lax.scan(step, state0, (u_t, dt_t, B_t, C_t))
            y = jnp.transpose(ys, (1, 0, 2))
            y = y * jax.nn.silu(z)
            return y @ out_w.T
        key = jax.random.key(seed)
        ks = jax.random.split(key, 10)
        inv = lambda n: 1.0 / np.sqrt(n)
        return {'x': jax.random.normal(ks[0], (BATCH, SEQ, D_MODEL), jnp.float32), 'in_proj_w': jax.random.uniform(ks[1], (2 * D_INNER, D_MODEL), jnp.float32, -inv(D_MODEL), inv(D_MODEL)), 'conv_w': jax.random.uniform(ks[2], (D_INNER, D_INNER, D_CONV), jnp.float32, -inv(D_INNER * D_CONV), inv(D_INNER * D_CONV)), 'conv_b': jax.random.uniform(ks[3], (D_INNER,), jnp.float32, -inv(D_INNER * D_CONV), inv(D_INNER * D_CONV)), 'dt_w': jax.random.uniform(ks[4], (D_INNER, D_INNER), jnp.float32, -inv(D_INNER), inv(D_INNER)), 'dt_b': jax.random.uniform(ks[5], (D_INNER,), jnp.float32, -inv(D_INNER), inv(D_INNER)), 'A_log': jax.random.normal(ks[6], (D_INNER, D_STATE), jnp.float32) * 0.01, 'D': jnp.ones((D_INNER,), jnp.float32), 'B_w': jax.random.uniform(ks[7], (D_STATE, D_INNER), jnp.float32, -inv(D_INNER), inv(D_INNER)), 'C_w': jax.random.uniform(ks[8], (D_STATE, D_INNER), jnp.float32, -inv(D_INNER), inv(D_INNER)), 'out_w': jax.random.uniform(ks[9], (D_MODEL, D_INNER), jnp.float32, -inv(D_INNER), inv(D_INNER))}
    _L0_attn_in = _L0_attn_setup()

    def _L0_ffn_setup():
        import jax, jax.numpy as jnp
        import numpy as np
        B, S, H = (2, 1024, 256)
        E, K, I = (8, 2, 352)
        key = jax.random.key(seed)
        ks = jax.random.split(key, 9)
        sc = 0.02
        return {'hidden_states': jax.random.normal(ks[0], (B, S, H), jnp.float32), 'gate_w': jax.random.normal(ks[1], (E, H), jnp.float32) * sc, 'w_gate': jax.random.normal(ks[2], (E, H, I), jnp.float32) * sc, 'w_up': jax.random.normal(ks[3], (E, H, I), jnp.float32) * sc, 'w_down': jax.random.normal(ks[4], (E, I, H), jnp.float32) * sc, 'sw_gate': jax.random.normal(ks[5], (H, I), jnp.float32) * sc, 'sw_up': jax.random.normal(ks[6], (H, I), jnp.float32) * sc, 'sw_down': jax.random.normal(ks[7], (I, H), jnp.float32) * sc, 'shared_gate_w': jax.random.normal(ks[8], (1, H), jnp.float32) * sc}
    _L0_ffn_in = _L0_ffn_setup()
    _d = {'L0_attn_x': _L0_attn_in['x'], 'L0_attn_in_proj_w': _L0_attn_in['in_proj_w'], 'L0_attn_conv_w': _L0_attn_in['conv_w'], 'L0_attn_conv_b': _L0_attn_in['conv_b'], 'L0_attn_dt_w': _L0_attn_in['dt_w'], 'L0_attn_dt_b': _L0_attn_in['dt_b'], 'L0_attn_A_log': _L0_attn_in['A_log'], 'L0_attn_D': _L0_attn_in['D'], 'L0_attn_B_w': _L0_attn_in['B_w'], 'L0_attn_C_w': _L0_attn_in['C_w'], 'L0_attn_out_w': _L0_attn_in['out_w'], 'L0_ffn_gate_w': _L0_ffn_in['gate_w'], 'L0_ffn_w_gate': _L0_ffn_in['w_gate'], 'L0_ffn_w_up': _L0_ffn_in['w_up'], 'L0_ffn_w_down': _L0_ffn_in['w_down'], 'L0_ffn_sw_gate': _L0_ffn_in['sw_gate'], 'L0_ffn_sw_up': _L0_ffn_in['sw_up'], 'L0_ffn_sw_down': _L0_ffn_in['sw_down'], 'L0_ffn_shared_gate_w': _L0_ffn_in['shared_gate_w']}
    _x0 = _d['L0_attn_x']
    _d['L0_attn_x'] = jax.random.normal(jax.random.fold_in(jax.random.key(seed), 1), (8, 1024, 256), dtype=_x0.dtype)
    del _x0
    return _d

def reference(L0_attn_x, L0_attn_in_proj_w, L0_attn_conv_w, L0_attn_conv_b, L0_attn_dt_w, L0_attn_dt_b, L0_attn_A_log, L0_attn_D, L0_attn_B_w, L0_attn_C_w, L0_attn_out_w, L0_ffn_gate_w, L0_ffn_w_gate, L0_ffn_w_up, L0_ffn_w_down, L0_ffn_sw_gate, L0_ffn_sw_up, L0_ffn_sw_down, L0_ffn_shared_gate_w):

    def _L0_attn_ref(x, in_proj_w, conv_w, conv_b, dt_w, dt_b, A_log, D, B_w, C_w, out_w):
        import jax, jax.numpy as jnp
        import numpy as np
        D_MODEL, D_STATE, D_CONV, EXPAND = (256, 16, 4, 2)
        D_INNER = EXPAND * D_MODEL
        BATCH, SEQ = (2, 512)

        def _forward(x, in_proj_w, conv_w, conv_b, dt_w, dt_b, A_log, D, B_w, C_w, out_w):
            xz = x @ in_proj_w.T
            xc, z = jnp.split(xz, 2, axis=-1)
            h = jnp.transpose(xc, (0, 2, 1))
            h = jnp.pad(h, ((0, 0), (0, 0), (D_CONV - 1, 0)))
            h = jax.lax.conv_general_dilated(h, conv_w, (1,), 'VALID', dimension_numbers=('NCH', 'OIH', 'NCH'))
            h = h + conv_b[None, :, None]
            u = jnp.transpose(h, (0, 2, 1))
            dt = jnp.clip(jax.nn.sigmoid(u @ dt_w.T + dt_b), 0.0001, 1.0)
            A = -jnp.exp(A_log)
            Bm = u @ B_w.T
            Cm = u @ C_w.T
            u_t = jnp.transpose(u, (1, 0, 2))
            dt_t = jnp.transpose(dt, (1, 0, 2))
            B_t = jnp.transpose(Bm, (1, 0, 2))
            C_t = jnp.transpose(Cm, (1, 0, 2))

            def step(state, inp):
                ut, dtt, bt, ct = inp
                dA = jnp.exp(jnp.clip(dtt[:, :, None] * A, -5.0, 5.0))
                dB = dtt[:, :, None] * bt[:, None, :] * ut[:, :, None]
                state = dA * state + dB + 1e-06
                y = jnp.sum(state * ct[:, None, :], axis=-1) + D * ut
                return (state, y)
            state0 = jnp.zeros((x.shape[0], D_INNER, D_STATE), x.dtype)
            _, ys = jax.lax.scan(step, state0, (u_t, dt_t, B_t, C_t))
            y = jnp.transpose(ys, (1, 0, 2))
            y = y * jax.nn.silu(z)
            return y @ out_w.T
        return _forward(x, in_proj_w, conv_w, conv_b, dt_w, dt_b, A_log, D, B_w, C_w, out_w)

    def _L0_ffn_ref(hidden_states, gate_w, w_gate, w_up, w_down, sw_gate, sw_up, sw_down, shared_gate_w):
        import jax, jax.numpy as jnp
        import numpy as np
        B, S, H = (2, 1024, 256)
        E, K, I = (8, 2, 352)
        b, s, h = hidden_states.shape
        x = hidden_states.reshape(-1, h)
        logits = jnp.einsum('th,eh->te', x, gate_w)
        probs = jax.nn.softmax(logits.astype(jnp.float32), axis=-1)
        topk_w, topk_i = jax.lax.top_k(probs, K)
        topk_w = topk_w / jnp.sum(topk_w, axis=-1, keepdims=True)
        combine = jnp.sum(jax.nn.one_hot(topk_i, E, dtype=topk_w.dtype) * topk_w[..., None], axis=1)
        combine = combine.astype(x.dtype)
        g = jnp.einsum('th,ehi->eti', x, w_gate)
        u = jnp.einsum('th,ehi->eti', x, w_up)
        eo = jnp.einsum('eti,eih->eth', jax.nn.silu(g) * u, w_down)
        out = jnp.einsum('te,eth->th', combine, eo)
        sg = jax.nn.sigmoid(jnp.einsum('th,oh->to', x, shared_gate_w))
        so = jax.nn.silu(x @ sw_gate) * (x @ sw_up) @ sw_down
        out = out + sg * so
        return out.reshape(b, s, h)
    x = L0_attn_x
    x = x + _L0_attn_ref(_layernorm(x, axis=-1), L0_attn_in_proj_w, L0_attn_conv_w, L0_attn_conv_b, L0_attn_dt_w, L0_attn_dt_b, L0_attn_A_log, L0_attn_D, L0_attn_B_w, L0_attn_C_w, L0_attn_out_w)
    x = x + _L0_ffn_ref(_layernorm(x, axis=-1), L0_ffn_gate_w, L0_ffn_w_gate, L0_ffn_w_up, L0_ffn_w_down, L0_ffn_sw_gate, L0_ffn_sw_up, L0_ffn_sw_down, L0_ffn_shared_gate_w)
    return x

_drawn_inputs = setup_inputs


def setup_inputs(seed=0):
    import zlib

    import numpy as np

    out = dict(_drawn_inputs(seed))
    spreads = {'L0_attn_D': (1.0, 0.6)}
    factors = {'L0_attn_conv_b': 8.0,
     'L0_attn_dt_w': 8.0,
     'L0_attn_dt_b': 8.0,
     'L0_attn_A_log': 8.0,
     'L0_attn_B_w': 8.0,
     'L0_attn_C_w': 8.0,
     'L0_ffn_gate_w': 4.6,
     'L0_ffn_w_gate': 4.048,
     'L0_ffn_w_up': 4.013,
     'L0_ffn_w_down': 4.004,
     'L0_ffn_sw_gate': 5.691,
     'L0_ffn_sw_up': 5.641,
     'L0_ffn_sw_down': 5.638,
     'L0_ffn_shared_gate_w': 8.0}
    for name, (base, spread) in spreads.items():
        noise = np.random.default_rng([zlib.crc32(name.encode()), seed]).standard_normal(out[name].shape)
        drawn = base * np.exp(spread * noise) if base else spread * noise
        out[name] = jnp.asarray(drawn.astype(out[name].dtype))
    for name, factor in factors.items():
        out[name] = (out[name] * factor).astype(out[name].dtype)
    return out
```

```python
from contextlib import ExitStack

import concourse.bass as bass
from concourse import mybir

F32 = mybir.dt.float32
I32 = mybir.dt.int32
U32 = mybir.dt.uint32
ALU = mybir.AluOpType
ACT = mybir.ActivationFunctionType
AX = mybir.AxisListType

BATCH, SEQ, DM = 8, 1024, 256
DI, NS, TAPS = 512, 16, 4
EXPERTS, HID = 8, 352
TOK = BATCH * SEQ
P = 128
TC = 256
CHUNKS = TOK // TC
PER_SEQ = SEQ // TC
NT = TC // P
KM = DM // P
KD = DI // P
FFNS = EXPERTS + 1
HB = 3
HROWS = [P, P, HID - 2 * P]
UNITS = FFNS * HB
HALO = TAPS - 1
NEAR = 4
PIECES = NS // NEAR
THRING = 2 * HB
LN_EPS, STATE_EPS, DT_MIN, DT_MAX, CLIP = 1e-5, 1e-6, 1e-4, 1.0, 5.0
CLIP_EXP = 0.006737946999085467

EVACS, PROJ_USES, POST_USES = 8, 10, 5
HEAD = 1


class Chunk:

    def __init__(self, pair, par):
        self.pair, self.par = pair, par
        self.index = pair * 2 + par

    def plus(self, n):
        k = self.par + n
        return Chunk(self.pair + k // 2, k % 2)

    def fixed(self):
        return isinstance(self.index, int)


def wait(eng, sem, value):
    if not isinstance(value, int) or value > 0:
        eng.wait_ge(sem, value)


FIRST_F = 4
UNIT_SLOT = [FIRST_F + u * (NS - FIRST_F) // UNITS for u in range(UNITS)]


def units_of(slot):
    return [u for u in range(UNITS) if UNIT_SLOT[u] == slot]


def build(nc, x, wx, wconv, wz, wdt, wbc, wout, conv_b, dt_b, d_skip, a_log, wgate, wgu, wd, out):
    x_v = x.rearrange("(c k p) d -> c p k d", p=P, k=NT)
    out_v = out.rearrange("(c k p) d -> c p k d", p=P, k=NT)
    b_scratch = nc.dram_tensor("b_scratch", [2, NS, TC], F32, kind="Internal").ap()

    ctx = ExitStack()
    with ctx:
        def sb(name, shape, dt=F32):
            return ctx.enter_context(nc.sbuf_tensor(name, shape, dt))

        def sem(name):
            return ctx.enter_context(nc.semaphore(name))

        w_gu = sb("w_gu", [P, FFNS, KM, 2 * HID])
        w_dn = sb("w_dn", [P, FFNS, HB, DM])
        w_conv = sb("w_conv", [P, TAPS, KM, DI])
        w_z = sb("w_z", [P, KM, DI])
        w_dt = sb("w_dt", [P, KD, DI])
        w_bc = sb("w_bc", [P, KD, 2 * NS])
        w_out = sb("w_out", [P, KD, DM])
        w_rt = sb("w_rt", [P, KM, FFNS])
        raw_conv = w_gu[:, 3:9, :, :].rearrange("p e k n -> p (e k n)")[:, 0:KD * TAPS * DI] \
            .rearrange("p (m t j) -> p m t j", m=KD, t=TAPS)
        raw_x = w_dn[:, 7:9, :, :].rearrange("p e k n -> p (e k n)")[:, 0:KD * DM] \
            .rearrange("p (m i) -> p m i", m=KD)

        ident = sb("ident", [P, P])
        diag_d = sb("diag_d", [P, KD, P])
        vec = sb("vec", [P, 3, KD])
        neg_dtb = sb("neg_dtb", [P, KD])
        a_raw = sb("a_raw", [P, KD, NS])
        a_exp = sb("a_exp", [P, KD, NS])
        neg_a = sb("neg_a", [P, KD, NS])
        a_max = sb("a_max", [P, 2])
        a_flag = sb("a_flag", [P, 1], I32)
        eps_col = sb("eps_col", [P, 1])
        neg_half = sb("neg_half", [P, NT])
        iota_i = sb("iota_i", [P, EXPERTS], I32)
        iota_f = sb("iota_f", [P, EXPERTS])
        mask = sb("mask", [P, 1])

        x_in = [sb(f"x_in{i}", [P, NT, DM]) for i in range(2)]
        p_st = sb("p_st", [P, NT, 6])
        p_mv = sb("p_mv", [P, NT, 2])
        p_var = sb("p_var", [P, NT])
        p_rstd = sb("p_rstd", [P, NT])
        xnT = sb("xnT", [P, KM, HALO + TC])
        uT = sb("uT", [P, KD, TC])
        b_row = sb("b_row", [NS, TC])
        dt = [sb(f"dt{i}", [P, KD, TC]) for i in range(2)]
        dtu = [sb(f"dtu{i}", [P, KD, TC]) for i in range(2)]
        zs = [sb(f"zs{i}", [P, NT, DI]) for i in range(2)]
        c_tok = [sb(f"c_tok{i}", [P, NT, NS]) for i in range(2)]
        acc = [sb(f"acc{i}", [P, NT, DI]) for i in range(2)]
        b_all = [sb(f"b_all{i}", [P, NEAR, TC]) for i in range(2)]
        v = [sb(f"v{i}", [P, KD, TC]) for i in range(2)]
        da = [sb(f"da{i}", [P, KD, TC]) for i in range(2)]
        carry = sb("carry", [P, NS, KD])
        yT = sb("yT", [P, KD, TC])
        x_res = sb("x_res", [P, NT, DM])
        x1 = [sb(f"x1_{i}", [P, NT, DM]) for i in range(2)]
        o_st = sb("o_st", [P, NT, 6])
        o_mv = sb("o_mv", [P, NT, 2])
        o_var = sb("o_var", [P, NT])
        o_rstd = sb("o_rstd", [P, NT])
        xn2 = sb("xn2", [P, NT, DM])
        xn2T = sb("xn2T", [P, KM, TC])
        lg = sb("lg", [P, NT, FFNS])
        top = sb("top", [P, NT, 8])
        top_i = sb("top_i", [P, NT, 8], U32)
        top_f = sb("top_f", [P, NT, 2])
        r_in = sb("r_in", [P, 2, NT])
        r_exp = sb("r_exp", [P, 2, NT])
        r_den = sb("r_den", [P, 2, NT])
        r_w = sb("r_w", [P, 2, NT])
        r_w2 = sb("r_w2", [P, NT])
        hot = sb("hot", [P, 2, NT, EXPERTS])
        comb = [sb(f"comb{i}", [P, NT, FFNS]) for i in range(2)]
        hid = sb("hid", [P, THRING, TC])
        up = sb("up", [P, 2, TC])

        banks = [ctx.enter_context(nc.psum_tensor(f"bank{i}", [P, 512], F32)) for i in range(8)]
        tr_bank, gu_bank, pr_bank, o_bank, dn_bank = banks[0:2], banks[2:4], banks[4:6], banks[6], banks[7]

        w_early = sem("w_early")
        w_raw = sem("w_raw")
        w_ffn = sem("w_ffn")
        pool_const = sem("pool_const")
        dve_const = sem("dve_const")
        a_exp_done = sem("a_exp_done")
        a_max_done = sem("a_max_done")
        comp_mm = sem("comp_mm")
        comp_done = sem("comp_done")
        x_loaded = [sem(f"x_loaded{i}") for i in range(2)]
        res_loaded = sem("res_loaded")
        out_done = [sem(f"out_done{i}") for i in range(2)]
        b_written = sem("b_written")
        b_loaded = [sem(f"b_loaded{i}") for i in range(2)]
        mask_done = sem("mask_done")
        norm_step = sem("norm_step")
        p_var_ready = sem("p_var_ready")
        p_rstd_ready = sem("p_rstd_ready")
        xn_ready = sem("xn_ready")
        pr_ready = sem("pr_ready")
        halo_done = sem("halo_done")
        evac = sem("evac")
        b_ready = sem("b_ready")
        zt_ready = sem("zt_ready")
        zs_done = sem("zs_done")
        dt_step = sem("dt_step")
        dt_ready = sem("dt_ready")
        dtu_ready = sem("dtu_ready")
        da_ready = sem("da_ready")
        v_mul = sem("v_mul")
        v_ready = sem("v_ready")
        clip_done = sem("clip_done")
        s_ready = sem("s_ready")
        carry_done = sem("carry_done")
        tr_ready = sem("tr_ready")
        cmul_done = sem("cmul_done")
        y_ready = sem("y_ready")
        o_ready = sem("o_ready")
        o_free = sem("o_free")
        x1_ready = sem("x1_ready")
        post_step = sem("post_step")
        o_var_ready = sem("o_var_ready")
        o_rstd_ready = sem("o_rstd_ready")
        xn2_ready = sem("xn2_ready")
        r_in_ready = sem("r_in_ready")
        r_exp_ready = sem("r_exp_ready")
        comb_ready = sem("comb_ready")
        gu_ready = sem("gu_ready")
        th_ready = sem("th_ready")
        up_ready = sem("up_ready")
        hg_ready = sem("hg_ready")
        h_ready = sem("h_ready")
        dn_ready = sem("dn_ready")
        mix_done = sem("mix_done")
        settled = sem("settled")
        sp_settled = sem("sp_settled")

        NORM_STEPS, DT_STEPS = 2 * NT, 2
        POST_STEPS = 1 + 2 * NT + NT + NT + 6 + 2 * NT
        EARLY_LOADS, RAW_LOADS, FFN_LOADS = 9, 2, 4

        def hid_slot(c, u):
            return (u + c.par * UNITS) % THRING

        def run(body):
            body.start()
            c0 = Chunk(0, 0)
            body(c0, None, c0.plus(1), c0.plus(2))
            with body.eng.Fori(0, (CHUNKS - 4) // 2) as i:
                for c in (Chunk(i, 1), Chunk(i, 1).plus(1)):
                    body(c, c.plus(-1), c.plus(1), c.plus(2))
            for n in range(CHUNKS - 3, CHUNKS + 1):
                c = Chunk(n // 2, n % 2)
                body(c if n < CHUNKS else None, c.plus(-1), c.plus(1) if n + 1 < CHUNKS else None,
                     c.plus(2) if n + 2 < CHUNKS else None)

        block = ctx.enter_context(nc.Block())

        @block.sync
        def _(sp):
            def sp_wait(sem_, value):
                wait(sp, sem_, value)
                sp.sem_inc(sp_settled, 1)

            def load_x(c):
                sp_wait(pr_ready, c.plus(-2).index * PROJ_USES + 1)
                sp.dma_start(x_in[c.par][:, :, :], x_v[c.index, :, :, :]).then_inc(x_loaded[c.par], 16)

            def load_res(c):
                sp_wait(x1_ready, c.index)
                sp.dma_start(x_res[:, :, :], x_v[c.index, :, :, :]).then_inc(res_loaded, 16)

            def write_b(c):
                sp_wait(b_ready, c.index + 1)
                sp_wait(b_loaded[0], c.plus(-1).index * 32)
                sp_wait(b_loaded[1], c.plus(-1).index * 32)
                sp.dma_start(b_scratch[c.par, :, :], b_row[:, :]).then_inc(b_written, 16)

            def load_b(c, p):
                sp_wait(b_written, c.index * 16 + 16)
                sp_wait(v_mul, c.index * NS + NEAR * (p - 1))
                src = b_scratch[c.par, NEAR * p:NEAR * (p + 1), :].rearrange("n t -> (n t)") \
                    .partition_broadcast(P)
                sp.dma_start(b_all[p % 2][:, :, :].rearrange("p n t -> p (n t)"), src) \
                  .then_inc(b_loaded[p % 2], 16)

            def store(c):
                sp_wait(mix_done, (c.index + 1) * FFNS + HEAD)
                sp.dma_start(out_v[c.index, :, :, :], x1[c.par][:, :, :]).then_inc(out_done[c.par], 16)

            class Body:
                eng = sp

                def start(self):
                    sp.sem_inc(out_done[0], 16)
                    sp.sem_inc(out_done[1], 16)
                    load_x(Chunk(0, 0))
                    load_x(Chunk(0, 1))
                    sp.dma_start(raw_x, wx).then_inc(w_raw, 16)
                    sp.dma_start(raw_conv, wconv).then_inc(w_raw, 16)
                    sp.dma_start(vec[:, 0, :], conv_b).then_inc(w_early, 16)
                    sp.dma_start(vec[:, 1, :], dt_b).then_inc(w_early, 16)
                    sp.dma_start(vec[:, 2, :], d_skip).then_inc(w_early, 16)
                    sp.dma_start(a_raw[:, :, :], a_log).then_inc(w_early, 16)
                    sp.dma_start(w_dt[:, :, :], wdt).then_inc(w_early, 16)
                    sp.dma_start(w_bc[:, :, :], wbc).then_inc(w_early, 16)
                    sp.dma_start(w_z[:, :, :], wz).then_inc(w_early, 16)
                    sp.dma_start(w_out[:, :, :], wout).then_inc(w_early, 16)
                    sp.dma_start(w_rt[:, :, :], wgate).then_inc(w_early, 16)
                    sp.dma_start(w_gu[:, 0:3, :, :], wgu[:, 0:3, :, :]).then_inc(w_ffn, 16)
                    sp.dma_start(w_dn[:, 0:7, :, :], wd[:, 0:7, :, :]).then_inc(w_ffn, 16)
                    sp.wait_ge(comp_mm, TAPS * KM)
                    sp.dma_start(w_gu[:, 3:FFNS, :, :], wgu[:, 3:FFNS, :, :]).then_inc(w_ffn, 16)
                    sp.dma_start(w_dn[:, 7:FFNS, :, :], wd[:, 7:FFNS, :, :]).then_inc(w_ffn, 16)
                    write_b(Chunk(0, 0))
                    load_b(Chunk(0, 0), 0)
                    load_b(Chunk(0, 0), 1)

                def __call__(self, scan, post, proj, norm):
                    if norm:
                        load_x(norm)
                    if scan:
                        load_res(scan)
                        load_b(scan, 2)
                    if proj:
                        write_b(proj)
                    if scan:
                        load_b(scan, 3)
                    if proj:
                        load_b(proj, 0)
                        load_b(proj, 1)
                    if post:
                        store(post)

            run(Body())
            sp.wait_ge(out_done[0], 16 * (CHUNKS // 2) + 16)
            sp.wait_ge(out_done[1], 16 * (CHUNKS // 2) + 16)

        @block.tensor
        def _(pe):
            mm = nc.tensor.matmul

            def transposes(bank, tiles):
                for n, tile in enumerate(tiles):
                    last = nc.tensor.transpose(bank[:, n * P:(n + 1) * P], tile, ident[:, :])
                return last

            def proj_norm(c):
                pe.wait_ge(xn_ready, c.index * NT + NT)
                wait(pe, evac, c.index * EVACS - 1)
                transposes(pr_bank[0], [x_in[c.par][:, k, b * P:(b + 1) * P] for b in range(KM) for k in range(NT)]) \
                    .then_inc(pr_ready, 1)

            def proj_conv(c, half):
                pe.wait_ge(evac, c.index * EVACS + 1)
                wait(pe, evac, c.index * EVACS + half)
                for j in range(2):
                    col = (2 * half + j) * P
                    for n, (t, b) in enumerate((t, b) for t in range(TAPS) for b in range(KM)):
                        last = mm(pr_bank[1 - half][:, j * TC:(j + 1) * TC], w_conv[:, t, b, col:col + P],
                                  xnT[:, b, t:t + TC], start=(n == 0), stop=(n == TAPS * KM - 1))
                last.then_inc(pr_ready, 1)

            def proj_dt(c, half):
                pe.wait_ge(evac, c.index * EVACS + 3)
                for j in range(2):
                    col = (2 * half + j) * P
                    for b in range(KD):
                        last = mm(pr_bank[1 - half][:, j * TC:(j + 1) * TC], w_dt[:, b, col:col + P],
                                  uT[:, b, :], start=(b == 0), stop=(b == KD - 1))
                last.then_inc(pr_ready, 1)

            def proj_bc(c):
                pe.wait_ge(evac, c.index * EVACS + 4)
                for b in range(KD):
                    mm(pr_bank[1][0:NS, 0:TC], w_bc[:, b, 0:NS], uT[:, b, :], start=(b == 0), stop=(b == KD - 1))
                for k in range(NT):
                    for b in range(KD):
                        last = mm(pr_bank[1][:, TC + k * NS:TC + (k + 1) * NS], uT[:, b, k * P:(k + 1) * P],
                                  w_bc[:, b, NS:2 * NS], start=(b == 0), stop=(b == KD - 1))
                last.then_inc(pr_ready, 1)

            def proj_z(c, k):
                pe.wait_ge(evac, c.index * EVACS + 5 + k)
                for b in range(KM):
                    last = mm(pr_bank[k][:, :], xnT[:, b, HALO + k * P:HALO + (k + 1) * P], w_z[:, b, :],
                              start=(b == 0), stop=(b == KM - 1))
                last.then_inc(pr_ready, 1)

            def proj_skip(c, k):
                pe.wait_ge(zs_done, c.index * NT + k + 1)
                for b in range(KD):
                    last = mm(pr_bank[k][:, b * P:(b + 1) * P], uT[:, b, k * P:(k + 1) * P], diag_d[:, b, :],
                              start=True, stop=True)
                last.then_inc(pr_ready, 1)

            def state_transpose(c, n):
                pe.wait_ge(s_ready, c.index * NS + n + 1)
                for k in range(NT):
                    wait(pe, cmul_done, c.index * NS * NT + NT * n + k - 1)
                    transposes(tr_bank[k], [v[n % 2][:, b, k * P:(k + 1) * P] for b in range(KD)]) \
                        .then_inc(tr_ready, 1)

            def post_y(c):
                pe.wait_ge(y_ready, c.index + 1)
                for h in range(2):
                    wait(pe, o_free, c.index * POST_USES + h + HEAD)
                    transposes(o_bank, [acc[c.par][:, k, b * P:(b + 1) * P]
                                        for b in (2 * h, 2 * h + 1) for k in range(NT)]).then_inc(o_ready, 1)

            def post_out(c):
                pe.wait_ge(o_free, c.index * POST_USES + 2 + HEAD)
                for k in range(NT):
                    for b in range(KD):
                        last = mm(o_bank[:, k * DM:(k + 1) * DM], yT[:, b, k * P:(k + 1) * P], w_out[:, b, :],
                                  start=(b == 0), stop=(b == KD - 1))
                last.then_inc(o_ready, 1)

            def post_norm(c):
                pe.wait_ge(xn2_ready, c.index * NT + NT)
                pe.wait_ge(o_free, c.index * POST_USES + 3 + HEAD)
                transposes(o_bank, [xn2[:, k, b * P:(b + 1) * P] for b in range(KM) for k in range(NT)]) \
                    .then_inc(o_ready, 1)

            def post_route(c):
                pe.wait_ge(o_free, c.index * POST_USES + 4 + HEAD)
                for k in range(NT):
                    for b in range(KM):
                        last = mm(o_bank[:, k * FFNS:(k + 1) * FFNS], xn2T[:, b, k * P:(k + 1) * P], w_rt[:, b, :],
                                  start=(b == 0), stop=(b == KM - 1))
                last.then_inc(o_ready, 1)

            def gate_up(c, u):
                e, m = divmod(u, HB)
                bank = gu_bank[(c.par + u) % 2]
                pe.wait_ge(hg_ready, c.index * UNITS + u + HEAD)
                pe.wait_ge(up_ready, c.index * UNITS + u + HEAD)
                rows = HROWS[m]
                for g in range(2):
                    col = g * HID + m * P
                    for b in range(KM):
                        last = mm(bank[0:rows, g * TC:(g + 1) * TC], w_gu[:, e, b, col:col + rows], xn2T[:, b, :],
                                  start=(b == 0), stop=(b == KM - 1))
                last.then_inc(gu_ready, 1)

            def down(c, e):
                pe.wait_ge(h_ready, c.index * UNITS + HB * e + HB + 1 + HEAD)
                wait(pe, mix_done, c.index * FFNS + e + HEAD)
                for k in range(NT):
                    for m in range(HB):
                        rows = HROWS[m]
                        last = mm(dn_bank[:, k * DM:(k + 1) * DM],
                                  hid[0:rows, hid_slot(c, HB * e + m), k * P:(k + 1) * P], w_dn[0:rows, e, m, :],
                                  start=(m == 0), stop=(m == HB - 1))
                last.then_inc(dn_ready, 1)

            def experts(c, slot):
                for u in units_of(slot):
                    gate_up(c, u)
                    if u % HB == HB - 1 and u >= 2 * HB - 1:
                        down(c, u // HB - 1)
                if slot == NS - 1:
                    down(c, FFNS - 1)

            def project(c, slot):
                if slot == 0:
                    proj_norm(c)
                    proj_conv(c, 0)
                if slot == 1:
                    proj_conv(c, 1)
                if slot == 2:
                    proj_dt(c, 0)
                    proj_dt(c, 1)
                if slot == 3:
                    proj_bc(c)
                    proj_z(c, 0)
                    proj_z(c, 1)
                if slot == 4:
                    proj_skip(c, 0)
                    proj_skip(c, 1)

            class Body:
                eng = pe

                def start(self):
                    pe.sem_inc(dn_ready, 1 + HEAD)
                    pe.wait_ge(w_raw, 16 * RAW_LOADS)
                    for t in range(TAPS):
                        for b in range(KM):
                            for m in range(KD):
                                last = mm(banks[t * KM + b][:, :], raw_x[:, m, b * P:(b + 1) * P],
                                          raw_conv[:, m, t, :], start=(m == 0), stop=(m == KD - 1))
                            last.then_inc(comp_mm, 1)
                    pe.wait_ge(comp_done, TAPS * KM)
                    pe.wait_ge(pool_const, 2)
                    pe.wait_ge(dve_const, 1)
                    pe.wait_ge(w_early, 16 * EARLY_LOADS)
                    for slot in range(5):
                        project(Chunk(0, 0), slot)
                    pe.wait_ge(w_ffn, 16 * FFN_LOADS)

                def __call__(self, scan, post, proj, norm):
                    for slot in range(NS):
                        if slot == 0 and post:
                            state_transpose(post, NS - 1)
                        if slot > 0 and scan:
                            state_transpose(scan, slot - 1)
                        if post and slot == 0:
                            post_y(post)
                        if post and slot == 1:
                            post_out(post)
                        if post and slot == 3:
                            post_norm(post)
                        if post and slot == 4:
                            post_route(post)
                        if proj:
                            project(proj, slot)
                        if post:
                            experts(post, slot)

            run(Body())

        @block.scalar
        def _(act):
            af = nc.scalar.activation

            def decays(c, n):
                if n == 0:
                    act.wait_ge(dt_ready, c.index + 1)
                wait(act, s_ready, c.index * NS + n - 1)
                for b in range(KD):
                    last = af(da[n % 2][:, b, :], dt[c.par][:, b, :], ACT.Exp, scale=neg_a[:, b, n:n + 1])
                last.then_inc(da_ready, 1)

            def add_eps(c, n):
                act.wait_ge(v_mul, c.index * NS + n + 1)
                af(v[n % 2][:, :, :], v[n % 2][:, :, :], ACT.Identity, bias=eps_col[:, 0:1]).then_inc(v_ready, 1)

            def project(c, slot):
                done = c.index * PROJ_USES
                if slot == 0:
                    act.wait_ge(pr_ready, done + 1)
                    if not (c.fixed() and c.index == 0):
                        tail = xnT[:, :, TC:TC + HALO]
                        if c.par == 0:
                            act.wait_ge(mask_done, c.pair)
                            af(xnT[:, :, 0:HALO], tail, ACT.Copy, scale=mask[:, 0:1]).then_inc(halo_done, 1)
                        else:
                            af(xnT[:, :, 0:HALO], tail, ACT.Copy).then_inc(halo_done, 1)
                        act.wait_ge(halo_done, c.index)
                    af(xnT[:, :, HALO:HALO + TC], pr_bank[0][:, :].rearrange("p (b t) -> p b t", b=KM), ACT.Copy) \
                        .then_inc(evac, 1)
                if slot in (0, 1):
                    act.wait_ge(pr_ready, done + 2 + slot)
                    for j in range(2):
                        b = 2 * slot + j
                        last = af(uT[:, b, :], pr_bank[1 - slot][:, j * TC:(j + 1) * TC], ACT.Identity,
                                  bias=vec[:, 0, b:b + 1])
                    last.then_inc(evac, 1)
                if slot == 2:
                    for h in range(2):
                        act.wait_ge(pr_ready, done + 4 + h)
                        for j in range(2):
                            b = 2 * h + j
                            last = af(dt[c.par][:, b, :], pr_bank[1 - h][:, j * TC:(j + 1) * TC], ACT.Exp,
                                      bias=neg_dtb[:, b:b + 1], scale=-1.0)
                        last.then_inc(evac, 1)
                if slot == 3:
                    act.wait_ge(pr_ready, done + 6)
                    wait(act, b_written, c.index * 16)
                    af(b_row[:, :], pr_bank[1][0:NS, 0:TC], ACT.Copy).then_inc(b_ready, 1)
                    af(c_tok[c.par][:, :, :], pr_bank[1][:, TC:TC + NT * NS].rearrange("p (k n) -> p k n", k=NT),
                       ACT.Copy).then_inc(evac, 1)
                    for k in range(NT):
                        act.wait_ge(pr_ready, done + 7 + k)
                        wait(act, y_ready, c.index - 1)
                        af(zs[c.par][:, k, :], pr_bank[k][:, :], ACT.Tanh, scale=0.5).then_inc(zt_ready, 1)
                if slot == 4:
                    for k in range(NT):
                        act.wait_ge(pr_ready, done + 9 + k)
                        af(acc[c.par][:, k, :], pr_bank[k][:, :], ACT.Copy).then_inc(evac, 1)

            def finish(c, slot):
                if slot == 0:
                    for h in range(2):
                        act.wait_ge(o_ready, c.index * POST_USES + h + 1)
                        af(yT[:, 2 * h:2 * h + 2, :], o_bank[:, :].rearrange("p (b t) -> p b t", b=2), ACT.Copy) \
                            .then_inc(o_free, 1)
                if slot == 3:
                    act.wait_ge(o_ready, c.index * POST_USES + 4)
                    af(xn2T[:, :, :], o_bank[:, :].rearrange("p (b t) -> p b t", b=KM), ACT.Copy).then_inc(o_free, 1)
                if slot == 4:
                    act.wait_ge(r_in_ready, c.index * 2 + 2)
                    af(r_exp[:, :, :], r_in[:, :, :], ACT.Exp).then_inc(r_exp_ready, 1)

            def gate(c, u):
                e, m = divmod(u, HB)
                rows = HROWS[m]
                bank = gu_bank[(c.par + u) % 2]
                act.wait_ge(gu_ready, c.index * UNITS + u + 1)
                act.wait_ge(dn_ready, c.index * FFNS + e + HEAD)
                af(hid[0:rows, hid_slot(c, u), :], bank[0:rows, 0:TC], ACT.Tanh, scale=0.5).then_inc(th_ready, 1)
                act.wait_ge(h_ready, c.index * UNITS + u + HEAD)
                af(up[0:rows, (c.par + u) % 2, :], bank[0:rows, TC:2 * TC], ACT.Copy).then_inc(up_ready, 1)

            class Body:
                eng = act

                def start(self):
                    act.sem_inc(up_ready, 1 + HEAD)
                    act.wait_ge(w_early, 16 * EARLY_LOADS)
                    af(a_exp[:, :, :], a_raw[:, :, :], ACT.Exp).then_inc(a_exp_done, 1)
                    for n in range(TAPS * KM):
                        act.wait_ge(comp_mm, n + 1)
                        af(w_conv[:, n // KM, n % KM, :], banks[n][:, :], ACT.Copy).then_inc(comp_done, 1)
                    act.wait_ge(pool_const, 4)
                    act.wait_ge(dve_const, 2)
                    for slot in range(5):
                        project(Chunk(0, 0), slot)
                    decays(Chunk(0, 0), 0)
                    add_eps(Chunk(0, 0), 0)

                def __call__(self, scan, post, proj, norm):
                    for slot in range(NS):
                        ahead = (scan, slot + 1) if slot + 1 < NS else (proj, 0)
                        if not scan:
                            ahead = (None, 0)
                        if ahead[0]:
                            decays(*ahead)
                        if post:
                            finish(post, slot)
                        if proj:
                            project(proj, slot)
                        now = units_of(slot) if post else []
                        for u in now[:1]:
                            gate(post, u)
                        if ahead[0]:
                            add_eps(*ahead)
                        for u in now[1:]:
                            gate(post, u)

            run(Body())

        @block.gpsimd
        def _(pool):
            def b_times_dtu(c, n):
                piece = n // NEAR
                if n == 0:
                    pool.wait_ge(dtu_ready, c.index + 1)
                if n % NEAR == 0:
                    pool.wait_ge(b_loaded[piece % 2], (c.index * 2 + piece // 2 + 1) * 16)
                wait(pool, tr_ready, c.index * NS * NT + NT * (n - 1))
                wait(pool, carry_done, c.index * NS + n - 1)
                row = b_all[piece % 2][:, n % NEAR:n % NEAR + 1, :].to_broadcast([P, KD, TC])
                nc.gpsimd.tensor_tensor(out=v[n % 2][:, :, :], in0=dtu[c.par][:, :, :], in1=row, op=ALU.mult) \
                    .then_inc(v_mul, 1)

            def rstd(out, var, ready, done, c):
                pool.wait_ge(ready, c.index + 1)
                nc.gpsimd.tensor_tensor(out=out[:, :], in0=var[:, :], in1=neg_half[:, :], op=ALU.pow) \
                    .then_inc(done, 1)

            def hidden(c, u):
                rows = HROWS[u % HB]
                pool.wait_ge(hg_ready, c.index * UNITS + u + 2 + HEAD)
                pool.wait_ge(up_ready, c.index * UNITS + u + 2 + HEAD)
                block_ = hid[0:rows, hid_slot(c, u), :]
                nc.gpsimd.tensor_tensor(out=block_, in0=block_, in1=up[0:rows, (c.par + u) % 2, :], op=ALU.mult) \
                    .then_inc(h_ready, 1)

            class Body:
                eng = pool

                def start(self):
                    pool.sem_inc(h_ready, 1 + HEAD)
                    nc.gpsimd.memset(ident[:, :], 0.0).then_inc(pool_const, 1)
                    pool.wait_ge(pool_const, 1)
                    nc.gpsimd.affine_select(out=ident[:, :], in_=ident[:, :], compare_op=ALU.not_equal, fill=1.0,
                                            base=0, pattern=[[-1, P]], channel_multiplier=1).then_inc(pool_const, 1)
                    nc.gpsimd.memset(eps_col[:, :], STATE_EPS).then_inc(pool_const, 1)
                    nc.gpsimd.memset(xnT[:, :, 0:HALO], 0.0).then_inc(pool_const, 1)
                    nc.gpsimd.memset(mask[:, :], 0.0).then_inc(pool_const, 1)
                    nc.gpsimd.iota(iota_i[:, :], pattern=[[1, EXPERTS]], base=0, channel_multiplier=0) \
                        .then_inc(pool_const, 1)
                    nc.gpsimd.memset(neg_half[:, :], -0.5).then_inc(pool_const, 1)
                    pool.wait_ge(pool_const, 7)
                    for n in range(2):
                        rstd(p_rstd, p_var, p_var_ready, p_rstd_ready, Chunk(0, n))
                    pool.wait_ge(dve_const, 3)
                    nc.gpsimd.partition_all_reduce(a_max[:, 1:2], a_max[:, 0:1], P, bass.bass_isa.ReduceOp.max) \
                        .then_inc(a_max_done, 1)
                    b_times_dtu(Chunk(0, 0), 0)

                def __call__(self, scan, post, proj, norm):
                    for slot in range(NS):
                        if scan and slot + 1 < NS:
                            b_times_dtu(scan, slot + 1)
                        if scan and proj and slot + 1 == NS:
                            b_times_dtu(proj, 0)
                        if post and slot == 1:
                            rstd(o_rstd, o_var, o_var_ready, o_rstd_ready, post)
                        if norm and slot == 12:
                            rstd(p_rstd, p_var, p_var_ready, p_rstd_ready, norm)
                        if post:
                            for u in units_of(slot):
                                hidden(post, u)

            run(Body())

        @block.vector
        def _(dve):
            vec_e = nc.vector

            def settle():
                dve.sem_inc(settled, 1)

            class Steps:

                def __init__(self, sem_, per, c):
                    self.sem, self.per, self.c, self.k = sem_, per, c, 0

                def did(self, ins):
                    self.k += 1
                    ins.then_inc(self.sem, 1)

                def sync(self):
                    dve.wait_ge(self.sem, self.c.index * self.per + self.k)

            def stats(c, src, st, mv, var, step, ready):
                for k in range(NT):
                    step.did(vec_e.bn_stats(st[:, k, :], src[:, k, :]))
                step.sync()
                settle()
                for k in range(NT):
                    step.did(vec_e.bn_aggr(mv[:, k, :], st[:, k, :]))
                step.sync()
                vec_e.tensor_scalar_add(var[:, :], mv[:, :, 1], LN_EPS).then_inc(ready, 1)

            def normed(dst, src, mv, rstd, ready):
                for k in range(NT):
                    vec_e.tensor_scalar(out=dst[:, k, :], in0=src[:, k, :], scalar1=mv[:, k, 0:1],
                                        scalar2=rstd[:, k:k + 1], op0=ALU.subtract, op1=ALU.mult).then_inc(ready, 1)

            def norm_stats(c):
                dve.wait_ge(x_loaded[c.par], c.pair * 16 + 16)
                stats(c, x_in[c.par], p_st, p_mv, p_var, Steps(norm_step, NORM_STEPS, c), p_var_ready)

            def norm_apply(c):
                dve.wait_ge(p_rstd_ready, c.index + 1)
                normed(x_in[c.par], x_in[c.par], p_mv, p_rstd, xn_ready)

            def proj_dt(c):
                dve.wait_ge(evac, c.index * EVACS + 5)
                step = Steps(dt_step, DT_STEPS, c)
                d = dt[c.par][:, :, :]
                step.did(vec_e.tensor_scalar_add(d, d, 1.0))
                step.sync()
                step.did(vec_e.reciprocal(d, d))
                step.sync()
                vec_e.tensor_scalar(out=d, in0=d, scalar1=DT_MIN, scalar2=DT_MAX, op0=ALU.max, op1=ALU.min) \
                    .then_inc(dt_ready, 1)
                dve.wait_ge(dt_ready, c.index + 1)
                vec_e.tensor_tensor(out=dtu[c.par][:, :, :], in0=d, in1=uT[:, :, :], op=ALU.mult) \
                    .then_inc(dtu_ready, 1)

            def proj_gate(c):
                for k in range(NT):
                    dve.wait_ge(zt_ready, c.index * NT + k + 1)
                    g = zs[c.par][:, k, :]
                    vec_e.scalar_tensor_tensor(out=g, in0=g, scalar=1.0, in1=pr_bank[k][:, :], op0=ALU.add,
                                               op1=ALU.mult).then_inc(zs_done, 1)

            def scans(c, n, flag):
                with dve.If(flag > 0):
                    dve.wait_ge(da_ready, c.index * NS + n + 1)
                    vec_e.tensor_scalar_max(da[n % 2][:, :, :], da[n % 2][:, :, :], CLIP_EXP).then_inc(clip_done, 1)
                    dve.wait_ge(clip_done, c.index * NS + n + 1)
                    settle()
                dve.wait_ge(da_ready, c.index * NS + n + 1)
                if n == 0:
                    wait(dve, carry_done, c.index * NS)
                dve.wait_ge(v_ready, c.index * NS + n + 1)
                for b in range(KD):
                    init = 0.0 if c.fixed() and c.index == 0 else carry[:, n, b:b + 1]
                    s = v[n % 2][:, b, :]
                    last = vec_e.tensor_tensor_scan(s, da[n % 2][:, b, :], s, init, ALU.mult, ALU.add)
                last.then_inc(s_ready, 1)

            def keep_last(c, n):
                dve.wait_ge(s_ready, c.index * NS + n + 1)
                src = v[n % 2][:, :, TC - 1]
                if c.par:
                    if n == 0:
                        dve.wait_ge(mask_done, c.pair + 1)
                    vec_e.tensor_scalar(out=carry[:, n, :], in0=src, scalar1=mask[:, 0:1], scalar2=None,
                                        op0=ALU.mult).then_inc(carry_done, 1)
                else:
                    vec_e.tensor_copy(carry[:, n, :], src).then_inc(carry_done, 1)

            def c_times_state(c, n):
                for k in range(NT):
                    if n == 0:
                        dve.wait_ge(evac, c.index * EVACS + 8)
                    dve.wait_ge(tr_ready, c.index * NS * NT + NT * n + k + 1)
                    if n > 0:
                        dve.wait_ge(cmul_done, c.index * NS * NT + NT * (n - 1) + k + 1)
                    a = acc[c.par][:, k, :]
                    vec_e.scalar_tensor_tensor(out=a, in0=tr_bank[k][:, :], scalar=c_tok[c.par][:, k, n:n + 1],
                                               in1=a, op0=ALU.mult, op1=ALU.add).then_inc(cmul_done, 1)

            def post_gate(c):
                dve.wait_ge(cmul_done, (c.index + 1) * NS * NT)
                dve.wait_ge(zs_done, (c.index + 1) * NT)
                a = acc[c.par][:, :, :]
                vec_e.scalar_tensor_tensor(out=a, in0=a, scalar=0.5, in1=zs[c.par][:, :, :], op0=ALU.mult,
                                           op1=ALU.mult).then_inc(y_ready, 1)

            def finish(c, slot, step):
                if slot == 0:
                    post_gate(c)
                if slot == 1:
                    dve.wait_ge(o_ready, c.index * POST_USES + 3)
                    dve.wait_ge(res_loaded, c.index * 16 + 16)
                    dve.wait_ge(out_done[c.par], c.pair * 16 + 16)
                    r = x1[c.par][:, :, :].rearrange("p k d -> p (k d)")
                    step.did(vec_e.tensor_tensor(out=r, in0=o_bank[:, :], in1=x_res[:, :, :]
                                                 .rearrange("p k d -> p (k d)"), op=ALU.add))
                    step.sync()
                    dve.sem_inc(x1_ready, 1)
                    dve.sem_inc(o_free, 1)
                    stats(c, x1[c.par], o_st, o_mv, o_var, step, o_var_ready)
                if slot == 2:
                    dve.wait_ge(o_rstd_ready, c.index + 1)
                    normed(xn2, x1[c.par], o_mv, o_rstd, xn2_ready)
                if slot == 4:
                    dve.wait_ge(o_ready, c.index * POST_USES + 5)
                    vec_e.tensor_copy(lg[:, :, :], o_bank[:, 0:NT * FFNS].rearrange("p (k e) -> p k e", k=NT)) \
                        .then_inc(o_free, 1)
                    dve.wait_ge(o_free, c.index * POST_USES + 5 + HEAD)
                    settle()
                    for k in range(NT):
                        step.did(vec_e.max(top[:, k, :], lg[:, k, 0:EXPERTS]))
                    step.sync()
                    vec_e.tensor_tensor(out=r_in[:, 0, :], in0=top[:, :, 1], in1=top[:, :, 0], op=ALU.subtract) \
                        .then_inc(r_in_ready, 1)
                    vec_e.tensor_scalar_mul(r_in[:, 1, :], lg[:, :, EXPERTS], -1.0).then_inc(r_in_ready, 1)
                    for k in range(NT):
                        step.did(vec_e.max_index(top_i[:, k, :], top[:, k, :], lg[:, k, 0:EXPERTS]))
                    step.sync()
                    step.did(vec_e.tensor_copy(top_f[:, :, :], top_i[:, :, 0:2]))
                    dve.wait_ge(r_exp_ready, c.index + 1)
                    step.did(vec_e.tensor_scalar_add(r_den[:, :, :], r_exp[:, :, :], 1.0))
                    step.sync()
                    step.did(vec_e.reciprocal(r_w[:, :, :], r_den[:, :, :]))
                    step.sync()
                    step.did(vec_e.tensor_scalar_mul(r_w[:, :, :], r_w[:, :, :], 0.5))
                    step.sync()
                    step.did(vec_e.tensor_tensor(out=r_w2[:, :], in0=r_exp[:, 0, :], in1=r_w[:, 0, :], op=ALU.mult))
                    step.did(vec_e.tensor_copy(comb[c.par][:, :, EXPERTS], r_w[:, 1, :]))
                    step.sync()
                    for k in range(NT):
                        step.did(vec_e.tensor_scalar(out=hot[:, 0, k, :], in0=iota_f[:, :], scalar1=top_f[:, k, 0:1],
                                                     scalar2=r_w[:, 0, k:k + 1], op0=ALU.is_equal, op1=ALU.mult))
                        step.did(vec_e.tensor_scalar(out=hot[:, 1, k, :], in0=iota_f[:, :], scalar1=top_f[:, k, 1:2],
                                                     scalar2=r_w2[:, k:k + 1], op0=ALU.is_equal, op1=ALU.mult))
                    step.sync()
                    vec_e.tensor_tensor(out=comb[c.par][:, :, 0:EXPERTS], in0=hot[:, 0, :, :], in1=hot[:, 1, :, :],
                                        op=ALU.add).then_inc(comb_ready, 1)
                    assert step.k == POST_STEPS, step.k

            def gated(c, u):
                rows = HROWS[u % HB]
                dve.wait_ge(th_ready, c.index * UNITS + u + 1)
                dve.wait_ge(up_ready, c.index * UNITS + u + 2 + HEAD)
                h = hid[0:rows, hid_slot(c, u), :]
                vec_e.scalar_tensor_tensor(out=h, in0=h, scalar=1.0, in1=gu_bank[(c.par + u) % 2][0:rows, 0:TC],
                                           op0=ALU.add, op1=ALU.mult).then_inc(hg_ready, 1)

            def mix(c, e):
                dve.wait_ge(dn_ready, c.index * FFNS + e + 2 + HEAD)
                if e == 0:
                    dve.wait_ge(comb_ready, c.index + 1)
                else:
                    dve.wait_ge(mix_done, c.index * FFNS + e + HEAD)
                for k in range(NT):
                    r = x1[c.par][:, k, :]
                    last = vec_e.scalar_tensor_tensor(out=r, in0=dn_bank[:, k * DM:(k + 1) * DM],
                                                      scalar=comb[c.par][:, k, e:e + 1], in1=r, op0=ALU.mult,
                                                      op1=ALU.add)
                last.then_inc(mix_done, 1)

            class Body:
                eng = dve

                def start(self):
                    dve.sem_inc(hg_ready, 1 + HEAD)
                    dve.sem_inc(o_free, HEAD)
                    dve.sem_inc(mix_done, HEAD)
                    dve.wait_ge(w_early, 16 * EARLY_LOADS)
                    dve.wait_ge(pool_const, 7)
                    for b in range(KD):
                        last = vec_e.tensor_scalar(out=diag_d[:, b, :], in0=ident[:, :], scalar1=vec[:, 2, b:b + 1],
                                                   scalar2=None, op0=ALU.mult)
                    last.then_inc(dve_const, 1)
                    vec_e.tensor_copy(iota_f[:, :], iota_i[:, :])
                    vec_e.tensor_scalar_mul(neg_dtb[:, :], vec[:, 1, :], -1.0)
                    dve.wait_ge(a_exp_done, 1)
                    vec_e.tensor_scalar_mul(neg_a[:, :, :], a_exp[:, :, :], -1.0).then_inc(dve_const, 1)
                    vec_e.reduce_max(a_max[:, 0:1], a_exp[:, :, :].rearrange("p b n -> p (b n)"), AX.X) \
                        .then_inc(dve_const, 1)
                    for n in range(2):
                        norm_stats(Chunk(0, n))
                        norm_apply(Chunk(0, n))
                    dve.wait_ge(a_max_done, 1)
                    vec_e.tensor_scalar(out=a_flag[:, :], in0=a_max[:, 1:2], scalar1=CLIP, scalar2=None,
                                        op0=ALU.is_gt).then_inc(dve_const, 1)
                    dve.wait_ge(dve_const, 4)
                    self.flag = dve.value_load(a_flag[0:1, 0:1], min_val=0, max_val=1)
                    proj_dt(Chunk(0, 0))
                    proj_gate(Chunk(0, 0))

                def __call__(self, scan, post, proj, norm):
                    step = Steps(post_step, POST_STEPS, post) if post else None
                    for slot in range(NS):
                        if slot == 0 and scan and scan.par:
                            vec_e.tensor_scalar(out=mask[:, :], in0=mask[:, :], scalar1=-1.0, scalar2=1.0,
                                                op0=ALU.mult, op1=ALU.add).then_inc(mask_done, 1)
                        if scan:
                            scans(scan, slot, self.flag)
                        if slot == 0 and post:
                            c_times_state(post, NS - 1)
                        if slot > 0 and scan:
                            c_times_state(scan, slot - 1)
                        if scan:
                            keep_last(scan, slot)
                        if post:
                            finish(post, slot, step)
                        if proj and slot == 3:
                            proj_dt(proj)
                            proj_gate(proj)
                        if norm and slot == 12:
                            norm_stats(norm)
                        if norm and slot == 13:
                            norm_apply(norm)
                        if post:
                            for u in units_of(slot):
                                gated(post, u)
                                if u >= 2 * HB and u % HB == 0:
                                    mix(post, u // HB - 2)
                            if slot == NS - 1:
                                mix(post, FFNS - 2)
                                mix(post, FFNS - 1)

            assert PER_SEQ == 4
            run(Body())


def kernel(**inputs):
    import numpy as np
    import concourse.bacc as bacc
    from concourse import mybir as _mybir
    from concourse.bass_utils import run_bass_kernel_spmd

    g = {k: np.asarray(v) for k, v in inputs.items()}
    cont = np.ascontiguousarray

    def rows(a):
        return cont(a.reshape(-1, P, a.shape[1]).transpose(1, 0, 2))

    def cols(a):
        return cont(np.moveaxis(a.reshape(-1, P, *a.shape[1:]), 0, 1))

    in_w = g["L0_attn_in_proj_w"]
    gu = np.concatenate([np.concatenate([g["L0_ffn_w_gate"], g["L0_ffn_w_up"]], axis=2),
                         np.concatenate([g["L0_ffn_sw_gate"], g["L0_ffn_sw_up"]], axis=1)[None]], axis=0)
    dn = np.concatenate([g["L0_ffn_w_down"], g["L0_ffn_sw_down"][None]], axis=0)
    dn = np.concatenate([dn, np.zeros((FFNS, HB * P - HID, DM), dn.dtype)], axis=1)
    arrays = {
        "x": cont(g["L0_attn_x"].reshape(TOK, DM)),
        "wx": rows(in_w[0:DI]),
        "wconv": cont(g["L0_attn_conv_w"].transpose(1, 2, 0).reshape(KD, P, TAPS, DI).transpose(1, 0, 2, 3)),
        "wz": rows(in_w[DI:2 * DI].T),
        "wdt": rows(g["L0_attn_dt_w"].T),
        "wbc": rows(np.concatenate([g["L0_attn_B_w"], g["L0_attn_C_w"]], axis=0).T),
        "wout": rows(g["L0_attn_out_w"].T),
        "conv_b": cols(g["L0_attn_conv_b"]),
        "dt_b": cols(g["L0_attn_dt_b"]),
        "d_skip": cols(g["L0_attn_D"]),
        "a_log": cols(g["L0_attn_A_log"]),
        "wgate": rows(np.concatenate([g["L0_ffn_gate_w"], g["L0_ffn_shared_gate_w"]], axis=0).T),
        "wgu": cont(gu.reshape(FFNS, KM, P, 2 * HID).transpose(2, 0, 1, 3)),
        "wd": cont(dn.reshape(FFNS, HB, P, DM).transpose(2, 0, 1, 3)),
    }
    nc = bacc.Bacc("TRN2", target_bir_lowering=False, num_devices=1)
    args = [nc.dram_tensor(f"in_{k}", a.shape, _mybir.dt.from_np(a.dtype), kind="ExternalInput").ap()
            for k, a in arrays.items()]
    out = nc.dram_tensor("out_0", (TOK, DM), F32, kind="ExternalOutput").ap()
    build(nc, *args, out)
    r = run_bass_kernel_spmd(nc, [{f"in_{k}": a for k, a in arrays.items()}], core_ids=[0])
    return r.results[0]["out_0"].reshape(BATCH, SEQ, DM)
```

```python
from contextlib import ExitStack

import concourse.bass as bass
from concourse import mybir

F32 = mybir.dt.float32
I32 = mybir.dt.int32
U32 = mybir.dt.uint32
ALU = mybir.AluOpType
ACT = mybir.ActivationFunctionType
AX = mybir.AxisListType

BATCH, SEQ, DM = 8, 1024, 256
DI, NS, TAPS = 512, 16, 4
EXPERTS, HID = 8, 352
TOK = BATCH * SEQ
P = 128
TC = 256
CHUNKS = TOK // TC
PER_SEQ = SEQ // TC
NT = TC // P
KM = DM // P
KD = DI // P
FFNS = EXPERTS + 1
HB = 3
HROWS = [P, P, HID - 2 * P]
UNITS = HB
PICKS = 2
TILE = TC
CAP = TOK + TILE
TILES = TOK * PICKS // TILE + EXPERTS
XG_ROWS = EXPERTS * CAP + TILE
Y_ROWS = TOK * PICKS + TILE
HALO = TAPS - 1
NEAR = 4
PIECES = NS // NEAR
THRING = 2 * HB
RING = 4
MUL_LEAD, DECAY_LEAD = 3, 2
ROW = DM + 4
LN_EPS, STATE_EPS, DT_MIN, DT_MAX, CLIP = 1e-5, 1e-6, 1e-4, 1.0, 5.0
CLIP_EXP = 0.006737946999085467

EVACS, PROJ_USES, POST_USES = 8, 10, 6
HEAD = 1


class Chunk:

    def __init__(self, pair, par):
        self.pair, self.par = pair, par
        self.index = pair * 2 + par

    def plus(self, n):
        k = self.par + n
        return Chunk(self.pair + k // 2, k % 2)

    def fixed(self):
        return isinstance(self.index, int)


def wait(eng, sem, value):
    if not isinstance(value, int) or value > 0:
        eng.wait_ge(sem, value)


UNIT_SLOT = [9, 10, 11]
DOWN_SLOT, MIX_SLOT = 13, 14


def units_of(slot):
    return [u for u in range(UNITS) if UNIT_SLOT[u] == slot]


def build(nc, x, wx, wconv, wz, wdt, wbc, wout, conv_b, dt_b, d_skip, a_log, wgate, wgu, wd, out):
    x_v = x.rearrange("(c k p) d -> c p k d", p=P, k=NT)
    out_v = out.rearrange("(c k p) d -> c p k d", p=P, k=NT)
    x1_s = nc.dram_tensor("x1_scratch", [CHUNKS, P, NT, DM], F32, kind="Internal").ap()
    xg = nc.dram_tensor("x_by_expert", [XG_ROWS, ROW], F32, kind="Internal").ap()
    y_s = nc.dram_tensor("y_by_token", [Y_ROWS, DM], F32, kind="Internal").ap()
    y_v = y_s[0:TOK * PICKS, :].rearrange("(c k p n) d -> c p k (n d)", p=P, k=NT, n=PICKS)
    b_scratch = nc.dram_tensor("b_scratch", [2, NS, TC], F32, kind="Internal").ap()

    ctx = ExitStack()
    with ctx:
        def sb(name, shape, dt=F32):
            return ctx.enter_context(nc.sbuf_tensor(name, shape, dt))

        def sem(name):
            return ctx.enter_context(nc.semaphore(name))

        w_gu = sb("w_gu", [P, KM, 2 * HID])
        w_dn = sb("w_dn", [P, HB, DM])
        w_conv = sb("w_conv", [P, TAPS, KM, DI])
        w_z = sb("w_z", [P, KM, DI])
        w_dt = sb("w_dt", [P, KD, DI])
        w_bc = sb("w_bc", [P, KD, 2 * NS])
        w_out = sb("w_out", [P, KD, DM])
        w_rt = sb("w_rt", [P, KM, FFNS])
        ident = sb("ident", [P, P])
        diag_d = sb("diag_d", [P, KD, P])
        vec = sb("vec", [P, 3, KD])
        a_raw = sb("a_raw", [P, KD, NS])
        a_exp = sb("a_exp", [P, KD, NS])
        neg_a = sb("neg_a", [P, KD, NS])
        a_max = sb("a_max", [P, 2])
        a_flag = sb("a_flag", [P, 1], I32)
        upper = sb("upper", [P, P])
        ones = sb("ones", [P, P])
        zeros = sb("zeros", [P, NT, ROW])
        step_i = sb("step_i", [P, TILES], I32)
        step_f = sb("step_f", [P, TILES])
        eps_col = sb("eps_col", [P, 1])
        neg_half = sb("neg_half", [P, NT])
        iota_i = sb("iota_i", [P, EXPERTS], I32)
        iota_f = sb("iota_f", [P, EXPERTS])
        mask = sb("mask", [P, 1])

        x_in = [sb(f"x_in{i}", [P, NT, DM]) for i in range(2)]
        p_st = sb("p_st", [P, NT, 6])
        p_mv = sb("p_mv", [P, NT, 2])
        p_var = sb("p_var", [P, NT])
        p_rstd = sb("p_rstd", [P, NT])
        xnT = sb("xnT", [P, KM, HALO + TC])
        uT = sb("uT", [P, KD, TC])
        b_row = sb("b_row", [NS, TC])
        dt = [sb(f"dt{i}", [P, KD, TC]) for i in range(2)]
        dtu = [sb(f"dtu{i}", [P, KD, TC]) for i in range(2)]
        zs = [sb(f"zs{i}", [P, NT, DI]) for i in range(2)]
        c_tok = [sb(f"c_tok{i}", [P, NT, NS]) for i in range(2)]
        acc = [sb(f"acc{i}", [P, NT, DI]) for i in range(2)]
        b_all = [sb(f"b_all{i}", [P, NEAR, TC]) for i in range(2)]
        v = [sb(f"v{i}", [P, KD, TC]) for i in range(RING)]
        da = [sb(f"da{i}", [P, KD, TC]) for i in range(RING)]
        carry = sb("carry", [P, NS, KD])
        yT = sb("yT", [P, KD, TC])
        x_res = sb("x_res", [P, NT, DM])
        x1 = [sb(f"x1_{i}", [P, NT, DM]) for i in range(2)]
        o_st = sb("o_st", [P, NT, 6])
        o_mv = sb("o_mv", [P, NT, 2])
        o_var = sb("o_var", [P, NT])
        o_rstd = sb("o_rstd", [P, NT])
        xn2 = [sb(f"xn2_{i}", [P, NT, ROW]) for i in range(2)]
        xn2T = sb("xn2T", [P, KM, TC])
        lg = sb("lg", [P, NT, FFNS])
        top = sb("top", [P, NT, 8])
        top_i = sb("top_i", [P, NT, 8], U32)
        top_f = sb("top_f", [P, NT, 2])
        r_in = sb("r_in", [P, 2, NT])
        r_exp = sb("r_exp", [P, 2, NT])
        r_den = sb("r_den", [P, 2, NT])
        r_w = sb("r_w", [P, 2, NT])
        w_sh = [sb(f"w_sh{i}", [P, NT]) for i in range(2)]
        w_all = sb("w_all", [P, CHUNKS, PICKS * NT])
        hot = sb("hot", [P, PICKS, NT, EXPERTS])
        sel = sb("sel", [P, NT, EXPERTS])
        row_of = sb("row_of", [P, NT, EXPERTS])
        picked = sb("picked", [P, PICKS, NT, EXPERTS])
        dest_f = sb("dest_f", [P, PICKS * NT])
        dest = [sb(f"dest{i}", [P, PICKS * NT], U32) for i in range(2)]
        home_i = sb("home_i", [P, NT], I32)
        home = sb("home", [P, NT])
        base = sb("base", [P, EXPERTS])
        first_row = sb("first_row", [P, EXPERTS])
        n_tok = sb("n_tok", [P, EXPERTS])
        n_gt = sb("n_gt", [P, EXPERTS, TOK // TILE])
        n_tiles = sb("n_tiles", [P, EXPERTS])
        n_incl = sb("n_incl", [P, EXPERTS])
        past = sb("past", [P, TILES, EXPERTS])
        past_t = sb("past_t", [P, TILES, EXPERTS])
        t_exp = sb("t_exp", [P, TILES])
        t_used = sb("t_used", [P, TILES])
        t_row = sb("t_row", [P, TILES])
        tab = sb("tab", [P, 2, TILES], I32)
        tab_zero = sb("tab_zero", [P, EXPERTS], I32)
        parts = [("t_gu", KM, 2 * HID), ("t_dn", HB, DM), ("xt", NT, ROW), ("xtT", KM, TILE), ("yt", NT, DM),
                 ("pick", NT, PICKS * DM)]
        late = sb("late", [P, 2 * sum(k * n for _, k, n in parts)])
        views, at = {}, 0
        for name, k, n in parts:
            views[name] = []
            for _ in range(2):
                views[name].append(late[:, at:at + k * n].rearrange("p (k n) -> p k n", k=k))
                at += k * n
        t_gu, t_dn, xt, xtT, yt, pick = (views[name] for name, _, _ in parts)
        raw_conv = late[:, 0:KD * TAPS * DI].rearrange("p (m t j) -> p m t j", m=KD, t=TAPS)
        raw_x = late[:, KD * TAPS * DI:KD * (TAPS * DI + DM)].rearrange("p (m i) -> p m i", m=KD)
        ids = [sb(f"ids{i}", [P, NT], U32) for i in range(2)]
        w_now = [sb(f"w_now{i}", [P, PICKS * NT]) for i in range(2)]
        hid = sb("hid", [P, THRING, TC])
        up = sb("up", [P, 2, TC])

        banks = [ctx.enter_context(nc.psum_tensor(f"bank{i}", [P, 512], F32)) for i in range(8)]
        tr_bank, gu_bank, pr_bank, o_bank, dn_bank = banks[0:2], banks[2:4], banks[4:6], banks[6], banks[7]

        w_early = sem("w_early")
        w_raw = sem("w_raw")
        pool_const = sem("pool_const")
        dve_const = sem("dve_const")
        a_exp_done = sem("a_exp_done")
        a_max_done = sem("a_max_done")
        comp_mm = sem("comp_mm")
        comp_done = sem("comp_done")
        x_loaded = [sem(f"x_loaded{i}") for i in range(2)]
        res_loaded = sem("res_loaded")
        out_done = [sem(f"out_done{i}") for i in range(2)]
        b_written = sem("b_written")
        b_loaded = [sem(f"b_loaded{i}") for i in range(2)]
        mask_done = sem("mask_done")
        norm_step = sem("norm_step")
        p_var_ready = sem("p_var_ready")
        p_rstd_ready = sem("p_rstd_ready")
        xn_ready = sem("xn_ready")
        pr_ready = sem("pr_ready")
        halo_done = sem("halo_done")
        evac = sem("evac")
        b_ready = sem("b_ready")
        zt_ready = sem("zt_ready")
        zs_done = sem("zs_done")
        dt_ready = sem("dt_ready")
        dtu_ready = sem("dtu_ready")
        da_ready = sem("da_ready")
        v_mul = sem("v_mul")
        v_ready = sem("v_ready")
        clip_done = sem("clip_done")
        s_ready = sem("s_ready")
        carry_done = sem("carry_done")
        tr_ready = sem("tr_ready")
        cmul_done = sem("cmul_done")
        y_ready = sem("y_ready")
        o_ready = sem("o_ready")
        o_free = sem("o_free")
        x1_ready = sem("x1_ready")
        post_step = sem("post_step")
        o_var_ready = sem("o_var_ready")
        o_rstd_ready = sem("o_rstd_ready")
        xn2_ready = sem("xn2_ready")
        r_in_ready = sem("r_in_ready")
        r_exp_ready = sem("r_exp_ready")
        sel_ready = sem("sel_ready")
        dest_ready = sem("dest_ready")
        scat_done = [sem(f"scat_done{i}") for i in range(2)]
        x1_stored = [sem(f"x1_stored{i}") for i in range(2)]
        table_step = sem("table_step")
        tab_ready = sem("tab_ready")
        zero_done = sem("zero_done")
        xt_loaded = [sem(f"xt_loaded{i}") for i in range(2)]
        gu_loaded = [sem(f"gu_loaded{i}") for i in range(2)]
        dn_loaded = [sem(f"dn_loaded{i}") for i in range(2)]
        ids_ready = sem("ids_ready")
        yt_ready = sem("yt_ready")
        sent = [sem(f"sent{i}") for i in range(2)]
        w_ready = sem("w_ready")
        pick_loaded = [sem(f"pick_loaded{i}") for i in range(2)]
        x1_loaded = [sem(f"x1_loaded{i}") for i in range(2)]
        pick_step = sem("pick_step")
        combined = sem("combined")
        gu_ready = sem("gu_ready")
        th_ready = sem("th_ready")
        up_ready = sem("up_ready")
        hg_ready = sem("hg_ready")
        h_ready = sem("h_ready")
        dn_ready = sem("dn_ready")
        mix_done = sem("mix_done")
        settled = sem("settled")
        pool_settled = sem("pool_settled")
        sp_settled = sem("sp_settled")

        NORM_STEPS = 2 * NT
        POST_STEPS = 1 + 2 * NT + (2 * NT + 1 + PICKS * NT) + 4 + (NT + 2) + 2
        EARLY_LOADS, RAW_LOADS = 11, 2

        def hid_slot(c, u):
            return (u + c.par * UNITS) % THRING

        def run(body):
            body.start()
            c0 = Chunk(0, 0)
            body(c0, None, c0.plus(1), c0.plus(2))
            with body.eng.Fori(0, (CHUNKS - 4) // 2) as i:
                for c in (Chunk(i, 1), Chunk(i, 1).plus(1)):
                    body(c, c.plus(-1), c.plus(1), c.plus(2))
            for n in range(CHUNKS - 3, CHUNKS + 1):
                c = Chunk(n // 2, n % 2)
                body(c if n < CHUNKS else None, c.plus(-1), c.plus(1) if n + 1 < CHUNKS else None,
                     c.plus(2) if n + 2 < CHUNKS else None)
            body.before_tiles()
            for par in range(2):
                body.tile(Chunk(0, par), False)
            with body.eng.Fori(1, TILES // 2 - 1) as i:
                for par in range(2):
                    body.tile(Chunk(i, par), False)
            for par in range(2):
                body.tile(Chunk(TILES // 2 - 1, par), par == 1)
            body.before_combine()
            for par in range(2):
                body.combine(Chunk(0, par))
            with body.eng.Fori(1, CHUNKS // 2) as i:
                for par in range(2):
                    body.combine(Chunk(i, par))

        def counted(t):
            return Chunk(t.pair + CHUNKS // 2, t.par)

        class Phases:
            def before_tiles(self):
                pass

            def before_combine(self):
                pass

        block = ctx.enter_context(nc.Block())

        @block.sync
        def _(sp):
            def sp_wait(sem_, value):
                wait(sp, sem_, value)
                sp.sem_inc(sp_settled, 1)

            def load_x(c):
                sp_wait(pr_ready, c.plus(-2).index * PROJ_USES + 1)
                sp.dma_start(x_in[c.par][:, :, :], x_v[c.index, :, :, :]).then_inc(x_loaded[c.par], 16)

            def load_res(c):
                sp_wait(x1_ready, c.index)
                sp.dma_start(x_res[:, :, :], x_v[c.index, :, :, :]).then_inc(res_loaded, 16)

            def write_b(c):
                sp_wait(b_ready, c.index + 1)
                sp_wait(b_loaded[0], c.plus(-1).index * 32)
                sp_wait(b_loaded[1], c.plus(-1).index * 32)
                sp.dma_start(b_scratch[c.par, :, :], b_row[:, :]).then_inc(b_written, 16)

            def load_b(c, p):
                sp_wait(b_written, c.index * 16 + 16)
                sp_wait(v_mul, c.index * NS + NEAR * (p - 1))
                src = b_scratch[c.par, NEAR * p:NEAR * (p + 1), :].rearrange("n t -> (n t)") \
                    .partition_broadcast(P)
                sp.dma_start(b_all[p % 2][:, :, :].rearrange("p n t -> p (n t)"), src) \
                  .then_inc(b_loaded[p % 2], 16)

            def store(c):
                sp_wait(mix_done, c.index + 1 + HEAD)
                sp.dma_start(x1_s[c.index, :, :, :], x1[c.par][:, :, :]).then_inc(x1_stored[c.par], 16)

            class Body(Phases):
                eng = sp

                def start(self):
                    for i in range(2):
                        sp.sem_inc(x1_stored[i], 16)
                    load_x(Chunk(0, 0))
                    load_x(Chunk(0, 1))
                    sp.dma_start(raw_x, wx).then_inc(w_raw, 16)
                    sp.dma_start(raw_conv, wconv).then_inc(w_raw, 16)
                    sp.dma_start(vec[:, 0, :], conv_b).then_inc(w_early, 16)
                    sp.dma_start(vec[:, 1, :], dt_b).then_inc(w_early, 16)
                    sp.dma_start(vec[:, 2, :], d_skip).then_inc(w_early, 16)
                    sp.dma_start(a_raw[:, :, :], a_log).then_inc(w_early, 16)
                    sp.dma_start(w_dt[:, :, :], wdt).then_inc(w_early, 16)
                    sp.dma_start(w_bc[:, :, :], wbc).then_inc(w_early, 16)
                    sp.dma_start(w_z[:, :, :], wz).then_inc(w_early, 16)
                    sp.dma_start(w_out[:, :, :], wout).then_inc(w_early, 16)
                    sp.dma_start(w_rt[:, :, :], wgate).then_inc(w_early, 16)
                    sp.dma_start(w_gu[:, :, :], wgu[EXPERTS, :, :, :]).then_inc(w_early, 16)
                    sp.dma_start(w_dn[:, :, :], wd[EXPERTS, :, :, :]).then_inc(w_early, 16)
                    write_b(Chunk(0, 0))
                    load_b(Chunk(0, 0), 0)
                    load_b(Chunk(0, 0), 1)

                def __call__(self, scan, post, proj, norm):
                    if norm:
                        load_x(norm)
                    if scan:
                        load_b(scan, 2)
                        load_res(scan)
                        load_b(scan, 3)
                    if proj:
                        write_b(proj)
                        load_b(proj, 0)
                        load_b(proj, 1)
                    if post:
                        store(post)

                def before_tiles(self):
                    sp.wait_ge(tab_ready, 1)
                    for e in range(EXPERTS):
                        row = sp.value_load(tab_zero[0:1, e:e + 1], min_val=0, max_val=XG_ROWS - TILE)
                        sp.dma_start(xg_rows(row), zeros[:, :, :]).then_inc(zero_done, 16)
                    sp.wait_ge(zero_done, 16 * EXPERTS)
                    for i in range(2):
                        sp.wait_ge(scat_done[i], CHUNKS // 2 * PICKS * NT * 16 + 16)

                    self.load_tokens(Chunk(0, 0))

                def load_tokens(self, t):
                    row = sp.value_load(tab[0:1, 1, bass.ds(t.index, 1)], min_val=0, max_val=XG_ROWS - TILE)
                    sp_wait(o_ready, POST_USES * CHUNKS + t.index - 1)
                    sp_wait(ids_ready, t.index - 1)
                    sp.dma_start(xt[t.par], xg_rows(row)).then_inc(xt_loaded[t.par], 16)

                def tile(self, t, last):
                    if not last:
                        self.load_tokens(t.plus(1))
                    j = t.index
                    e = sp.value_load(tab[0:1, 0, bass.ds(j, 1)], min_val=0, max_val=EXPERTS)
                    sp_wait(gu_ready, (counted(t).index - 1) * UNITS)
                    sp.dma_start(t_gu[t.par], wgu[bass.ds(e, 1), :, :, :].rearrange("a p k n -> (a p) k n")) \
                      .then_inc(gu_loaded[t.par], 16)
                    sp_wait(dn_ready, counted(t).index + HEAD)
                    sp.dma_start(t_dn[t.par], wd[bass.ds(e, 1), :, :, :].rearrange("a p k n -> (a p) k n")) \
                      .then_inc(dn_loaded[t.par], 16)

                def combine(self, c):
                    sp_wait(combined, c.index + 1)
                    sp.dma_start(out_v[c.index, :, :, :], x1[c.par][:, :, :]).then_inc(out_done[c.par], 16)

            def xg_rows(row):
                return xg[bass.ds(row, TILE), :].rearrange("(k p) d -> p k d", p=P)

            run(Body())
            sp.wait_ge(out_done[0], 16 * (CHUNKS // 2))
            sp.wait_ge(out_done[1], 16 * (CHUNKS // 2))

        @block.tensor
        def _(pe):
            mm = nc.tensor.matmul

            def transposes(bank, tiles):
                for n, tile in enumerate(tiles):
                    last = nc.tensor.transpose(bank[:, n * P:(n + 1) * P], tile, ident[:, :])
                return last

            def proj_norm(c):
                pe.wait_ge(xn_ready, c.index * NT + NT)
                wait(pe, evac, c.index * EVACS - 1)
                transposes(pr_bank[0], [x_in[c.par][:, k, b * P:(b + 1) * P] for b in range(KM) for k in range(NT)]) \
                    .then_inc(pr_ready, 1)

            def proj_conv(c, half, j):
                pe.wait_ge(evac, c.index * EVACS + 1)
                col = (2 * half + j) * P
                for n, (t, b) in enumerate((t, b) for t in range(TAPS) for b in range(KM)):
                    last = mm(pr_bank[1 - half][:, j * TC:(j + 1) * TC], w_conv[:, t, b, col:col + P],
                              xnT[:, b, t:t + TC], start=(n == 0), stop=(n == TAPS * KM - 1))
                if j == 1:
                    last.then_inc(pr_ready, 1)

            def proj_dt(c, half):
                pe.wait_ge(evac, c.index * EVACS + 3)
                for j in range(2):
                    col = (2 * half + j) * P
                    for b in range(KD):
                        last = mm(pr_bank[1 - half][:, j * TC:(j + 1) * TC], w_dt[:, b, col:col + P],
                                  uT[:, b, :], start=(b == 0), stop=(b == KD - 1))
                last.then_inc(pr_ready, 1)

            def proj_bc(c):
                pe.wait_ge(evac, c.index * EVACS + 4)
                for b in range(KD):
                    mm(pr_bank[1][0:NS, 0:TC], w_bc[:, b, 0:NS], uT[:, b, :], start=(b == 0), stop=(b == KD - 1))
                for k in range(NT):
                    for b in range(KD):
                        last = mm(pr_bank[1][:, TC + k * NS:TC + (k + 1) * NS], uT[:, b, k * P:(k + 1) * P],
                                  w_bc[:, b, NS:2 * NS], start=(b == 0), stop=(b == KD - 1))
                last.then_inc(pr_ready, 1)

            def proj_z(c, k):
                pe.wait_ge(evac, c.index * EVACS + 5 + k)
                for b in range(KM):
                    last = mm(pr_bank[k][:, :], xnT[:, b, HALO + k * P:HALO + (k + 1) * P], w_z[:, b, :],
                              start=(b == 0), stop=(b == KM - 1))
                last.then_inc(pr_ready, 1)

            def proj_skip(c, k):
                pe.wait_ge(zs_done, c.index * NT + k + 1)
                for b in range(KD):
                    last = mm(pr_bank[k][:, b * P:(b + 1) * P], uT[:, b, k * P:(k + 1) * P], diag_d[:, b, :],
                              start=True, stop=True)
                last.then_inc(pr_ready, 1)

            def state_transpose(c, n):
                pe.wait_ge(s_ready, c.index * NS + n + 1)
                for k in range(NT):
                    wait(pe, cmul_done, c.index * NS * NT + NT * n + k - 1)
                    transposes(tr_bank[k], [v[n % RING][:, b, k * P:(k + 1) * P] for b in range(KD)]) \
                        .then_inc(tr_ready, 1)

            def post_y(c, h):
                pe.wait_ge(y_ready, c.index + 1)
                wait(pe, o_free, c.index * POST_USES + h + HEAD)
                transposes(o_bank, [acc[c.par][:, k, b * P:(b + 1) * P]
                                    for b in (2 * h, 2 * h + 1) for k in range(NT)]).then_inc(o_ready, 1)

            def post_out(c):
                pe.wait_ge(o_free, c.index * POST_USES + 2 + HEAD)
                for k in range(NT):
                    for b in range(KD):
                        last = mm(o_bank[:, k * DM:(k + 1) * DM], yT[:, b, k * P:(k + 1) * P], w_out[:, b, :],
                                  start=(b == 0), stop=(b == KD - 1))
                last.then_inc(o_ready, 1)

            def post_norm(c):
                pe.wait_ge(xn2_ready, c.index * NT + NT)
                pe.wait_ge(o_free, c.index * POST_USES + 3 + HEAD)
                transposes(o_bank, [xn2[c.par][:, k, b * P:(b + 1) * P] for b in range(KM) for k in range(NT)]) \
                    .then_inc(o_ready, 1)

            def post_route(c):
                pe.wait_ge(o_free, c.index * POST_USES + 4 + HEAD)
                for k in range(NT):
                    for b in range(KM):
                        last = mm(o_bank[:, k * FFNS:(k + 1) * FFNS], xn2T[:, b, k * P:(k + 1) * P], w_rt[:, b, :],
                                  start=(b == 0), stop=(b == KM - 1))
                last.then_inc(o_ready, 1)

            def post_rank(c):
                pe.wait_ge(sel_ready, c.index + 1)
                for k in range(NT + 1):
                    for b in range(min(k + 1, NT)):
                        last = mm(o_bank[:, k * EXPERTS:(k + 1) * EXPERTS], (upper if b == k else ones)[:, :],
                                  sel[:, b, :], start=(b == 0), stop=(b == min(k, NT - 1)))
                last.then_inc(o_ready, 1)

            def gate_up(c, u, w, xT):
                bank = gu_bank[(c.par + u) % 2]
                pe.wait_ge(hg_ready, c.index * UNITS + u + HEAD)
                pe.wait_ge(up_ready, c.index * UNITS + u + HEAD)
                rows = HROWS[u]
                for g in range(2):
                    col = g * HID + u * P
                    for b in range(KM):
                        last = mm(bank[0:rows, g * TC:(g + 1) * TC], w[:, b, col:col + rows], xT[:, b, :],
                                  start=(b == 0), stop=(b == KM - 1))
                last.then_inc(gu_ready, 1)

            def down(c, w):
                pe.wait_ge(h_ready, c.index * UNITS + HB + 1 + HEAD)
                pe.wait_ge(mix_done, c.index + HEAD)
                for k in range(NT):
                    for m in range(HB):
                        rows = HROWS[m]
                        last = mm(dn_bank[:, k * DM:(k + 1) * DM],
                                  hid[0:rows, hid_slot(c, m), k * P:(k + 1) * P], w[0:rows, m, :],
                                  start=(m == 0), stop=(m == HB - 1))
                last.then_inc(dn_ready, 1)

            def tile_transpose(t):
                pe.wait_ge(xt_loaded[t.par], t.pair * 16 + 16)
                pe.wait_ge(o_free, CHUNKS * POST_USES + t.index + HEAD)
                transposes(o_bank, [xt[t.par][:, k, b * P:(b + 1) * P] for b in range(KM) for k in range(NT)]) \
                    .then_inc(o_ready, 1)

            def project(c, slot):
                if slot < 4:
                    proj_conv(c, slot // 2, slot % 2)
                if slot in (5, 6):
                    proj_dt(c, slot - 5)
                if slot == 8:
                    proj_bc(c)
                if slot in (9, 10):
                    proj_z(c, slot - 9)
                if slot in (11, 12):
                    proj_skip(c, slot - 11)

            class Body(Phases):
                eng = pe

                def start(self):
                    pe.sem_inc(dn_ready, 1 + HEAD)
                    pe.wait_ge(w_raw, 16 * RAW_LOADS)
                    for t in range(TAPS):
                        for b in range(KM):
                            for m in range(KD):
                                last = mm(banks[t * KM + b][:, :], raw_x[:, m, b * P:(b + 1) * P],
                                          raw_conv[:, m, t, :], start=(m == 0), stop=(m == KD - 1))
                            last.then_inc(comp_mm, 1)
                    pe.wait_ge(comp_done, TAPS * KM)
                    pe.wait_ge(pool_const, 11)
                    pe.wait_ge(dve_const, 1)
                    pe.wait_ge(w_early, 16 * EARLY_LOADS)
                    proj_norm(Chunk(0, 0))
                    for slot in range(NS):
                        project(Chunk(0, 0), slot)
                    proj_norm(Chunk(0, 1))

                def __call__(self, scan, post, proj, norm):
                    for slot in range(NS):
                        if slot == 0 and post:
                            state_transpose(post, NS - 1)
                        if slot > 0 and scan:
                            state_transpose(scan, slot - 1)
                        if post and slot in (1, 2):
                            post_y(post, slot - 1)
                        if post and slot == 4:
                            post_out(post)
                        if post and slot == 7:
                            post_norm(post)
                        if post and slot == 8:
                            post_route(post)
                        if post and slot == 10:
                            post_rank(post)
                        if proj:
                            project(proj, slot)
                        if norm and slot == NS - 1:
                            proj_norm(norm)
                        if post:
                            for u in units_of(slot):
                                gate_up(post, u, w_gu, xn2T)
                            if slot == DOWN_SLOT:
                                down(post, w_dn)

                def before_tiles(self):
                    tile_transpose(Chunk(0, 0))

                def tile(self, t, last):
                    c = counted(t)
                    pe.wait_ge(o_free, CHUNKS * POST_USES + t.index + 1 + HEAD)
                    pe.wait_ge(gu_loaded[t.par], t.pair * 16 + 16)
                    gate_up(c, 0, t_gu[t.par], xtT[t.par])
                    if not last:
                        tile_transpose(t.plus(1))
                    gate_up(c, 1, t_gu[t.par], xtT[t.par])
                    if not (t.fixed() and t.index == 0):
                        self.tile_down(t.plus(-1))
                    gate_up(c, 2, t_gu[t.par], xtT[t.par])
                    if last:
                        self.tile_down(t)

                def tile_down(self, t):
                    pe.wait_ge(dn_loaded[t.par], t.pair * 16 + 16)
                    down(counted(t), t_dn[t.par])

                def combine(self, c):
                    pass

            run(Body())

        @block.scalar
        def _(act):
            af = nc.scalar.activation

            def decays(c, n):
                if n == 0:
                    act.wait_ge(dt_ready, c.index + 1)
                wait(act, s_ready, c.index * NS + n - RING + 1)
                for b in range(KD):
                    last = af(da[n % RING][:, b, :], dt[c.par][:, b, :], ACT.Exp, scale=neg_a[:, b, n:n + 1])
                last.then_inc(da_ready, 1)

            def add_eps(c, n):
                act.wait_ge(v_mul, c.index * NS + n + 1)
                af(v[n % RING][:, :, :], v[n % RING][:, :, :], ACT.Identity, bias=eps_col[:, 0:1]).then_inc(v_ready, 1)

            def take_normed(c):
                act.wait_ge(pr_ready, c.index * PROJ_USES + 1)
                if not (c.fixed() and c.index == 0):
                    tail = xnT[:, :, TC:TC + HALO]
                    if c.par == 0:
                        act.wait_ge(mask_done, c.pair)
                        af(xnT[:, :, 0:HALO], tail, ACT.Copy, scale=mask[:, 0:1]).then_inc(halo_done, 1)
                    else:
                        af(xnT[:, :, 0:HALO], tail, ACT.Copy).then_inc(halo_done, 1)
                    act.wait_ge(halo_done, c.index)
                af(xnT[:, :, HALO:HALO + TC], pr_bank[0][:, :].rearrange("p (b t) -> p b t", b=KM), ACT.Copy) \
                    .then_inc(evac, 1)

            def project(c, slot):
                done = c.index * PROJ_USES
                if slot in (2, 4):
                    h = slot // 2 - 1
                    act.wait_ge(pr_ready, done + 2 + h)
                    for j in range(2):
                        b = 2 * h + j
                        last = af(uT[:, b, :], pr_bank[1 - h][:, j * TC:(j + 1) * TC], ACT.Identity,
                                  bias=vec[:, 0, b:b + 1])
                    last.then_inc(evac, 1)
                if slot == 7:
                    for h in range(2):
                        act.wait_ge(pr_ready, done + 4 + h)
                        for j in range(2):
                            b = 2 * h + j
                            last = af(dt[c.par][:, b, :], pr_bank[1 - h][:, j * TC:(j + 1) * TC], ACT.Sigmoid,
                                      bias=vec[:, 1, b:b + 1])
                        last.then_inc(evac, 1)
                if slot == 8:
                    act.wait_ge(pr_ready, done + 6)
                    wait(act, b_written, c.index * 16)
                    af(b_row[:, :], pr_bank[1][0:NS, 0:TC], ACT.Copy).then_inc(b_ready, 1)
                    af(c_tok[c.par][:, :, :], pr_bank[1][:, TC:TC + NT * NS].rearrange("p (k n) -> p k n", k=NT),
                       ACT.Copy).then_inc(evac, 1)
                if slot in (9, 10):
                    k = slot - 9
                    act.wait_ge(pr_ready, done + 7 + k)
                    wait(act, y_ready, c.index - 1)
                    af(zs[c.par][:, k, :], pr_bank[k][:, :], ACT.Tanh, scale=0.5).then_inc(zt_ready, 1)
                if slot in (12, 13):
                    k = slot - 12
                    act.wait_ge(pr_ready, done + 9 + k)
                    af(acc[c.par][:, k, :], pr_bank[k][:, :], ACT.Copy).then_inc(evac, 1)

            def finish(c, slot):
                if slot in (1, 2):
                    h = slot - 1
                    act.wait_ge(o_ready, c.index * POST_USES + h + 1)
                    af(yT[:, 2 * h:2 * h + 2, :], o_bank[:, :].rearrange("p (b t) -> p b t", b=2), ACT.Copy) \
                        .then_inc(o_free, 1)
                if slot == 7:
                    act.wait_ge(o_ready, c.index * POST_USES + 4)
                    af(xn2T[:, :, :], o_bank[:, :].rearrange("p (b t) -> p b t", b=KM), ACT.Copy).then_inc(o_free, 1)
                if slot == 10:
                    act.wait_ge(r_in_ready, c.index * 2 + 2)
                    af(r_exp[:, :, :], r_in[:, :, :], ACT.Exp).then_inc(r_exp_ready, 1)

            def gate(c, u):
                rows = HROWS[u]
                bank = gu_bank[(c.par + u) % 2]
                act.wait_ge(gu_ready, c.index * UNITS + u + 1)
                act.wait_ge(dn_ready, c.index + HEAD)
                af(hid[0:rows, hid_slot(c, u), :], bank[0:rows, 0:TC], ACT.Tanh, scale=0.5).then_inc(th_ready, 1)
                act.wait_ge(h_ready, c.index * UNITS + u + HEAD)
                af(up[0:rows, (c.par + u) % 2, :], bank[0:rows, TC:2 * TC], ACT.Copy).then_inc(up_ready, 1)

            class Body(Phases):
                eng = act

                def start(self):
                    act.sem_inc(up_ready, 1 + HEAD)
                    act.wait_ge(w_early, 16 * EARLY_LOADS)
                    af(a_exp[:, :, :], a_raw[:, :, :], ACT.Exp).then_inc(a_exp_done, 1)
                    for n in range(TAPS * KM):
                        act.wait_ge(comp_mm, n + 1)
                        af(w_conv[:, n // KM, n % KM, :], banks[n][:, :], ACT.Copy).then_inc(comp_done, 1)
                    act.wait_ge(pool_const, 11)
                    act.wait_ge(dve_const, 3)
                    take_normed(Chunk(0, 0))
                    for slot in range(NS):
                        project(Chunk(0, 0), slot)
                    take_normed(Chunk(0, 1))
                    for n in range(DECAY_LEAD):
                        decays(Chunk(0, 0), n)
                        add_eps(Chunk(0, 0), n)

                def __call__(self, scan, post, proj, norm):
                    for slot in range(NS):
                        n = slot + DECAY_LEAD
                        ahead = (None, 0) if not scan else (scan, n) if n < NS else (proj, n - NS)
                        if ahead[0]:
                            decays(*ahead)
                            add_eps(*ahead)
                        if post:
                            finish(post, slot)
                        if proj:
                            project(proj, slot)
                        if post:
                            for u in units_of(slot):
                                gate(post, u)
                        if norm and slot == NS - 1:
                            take_normed(norm)

                def before_tiles(self):
                    self.turned(Chunk(0, 0))

                def turned(self, t):
                    act.wait_ge(o_ready, CHUNKS * POST_USES + t.index + 1)
                    af(xtT[t.par], o_bank[:, :].rearrange("p (b t) -> p b t", b=KM), ACT.Copy).then_inc(o_free, 1)

                def tile(self, t, last):
                    c = counted(t)
                    gate(c, 0)
                    if not last:
                        self.turned(t.plus(1))
                    gate(c, 1)
                    if not (t.fixed() and t.index == 0):
                        self.tile_out(t.plus(-1))
                    gate(c, 2)
                    if last:
                        self.tile_out(t)

                def tile_out(self, t):
                    act.wait_ge(dn_ready, counted(t).index + 2 + HEAD)
                    if not (t.fixed() and t.pair == 0):
                        act.wait_ge(sent[t.par], t.pair * NT * 16)
                    af(yt[t.par], dn_bank[:, :].rearrange("p (k d) -> p k d", k=NT), ACT.Copy).then_inc(yt_ready, 1)
                    act.wait_ge(yt_ready, t.index + 1)
                    act.sem_inc(mix_done, 1)

                def before_combine(self):
                    for i in range(2):
                        act.wait_ge(x1_stored[i], 16 * (CHUNKS // 2) + 16)
                        act.wait_ge(sent[i], 16 * NT * (TILES // 2))

                def combine(self, c):
                    wait(act, out_done[c.par], c.pair * 16)
                    act.dma_start(x1[c.par][:, :, :], x1_s[c.index, :, :, :]).then_inc(x1_loaded[c.par], 16)
                    act.dma_start(pick[c.par], y_v[c.index, :, :, :]).then_inc(pick_loaded[c.par], 16)

            run(Body())

        @block.gpsimd
        def _(pool):
            def b_times_dtu(c, n):
                piece = n // NEAR
                if n == 0:
                    pool.wait_ge(dtu_ready, c.index + 1)
                if n % NEAR == 0:
                    pool.wait_ge(b_loaded[piece % 2], (c.index * 2 + piece // 2 + 1) * 16)
                wait(pool, tr_ready, c.index * NS * NT + NT * (n - RING + 1))
                wait(pool, carry_done, c.index * NS + n - RING + 1)
                row = b_all[piece % 2][:, n % NEAR:n % NEAR + 1, :].to_broadcast([P, KD, TC])
                nc.gpsimd.tensor_tensor(out=v[n % RING][:, :, :], in0=dtu[c.par][:, :, :], in1=row, op=ALU.mult) \
                    .then_inc(v_mul, 1)

            def rstd(out, var, ready, done, c):
                pool.wait_ge(ready, c.index + 1)
                nc.gpsimd.tensor_tensor(out=out[:, :], in0=var[:, :], in1=neg_half[:, :], op=ALU.pow) \
                    .then_inc(done, 1)

            def scatter(c, n):
                pool.wait_ge(dest_ready, c.index * 2 + n + 1)
                pool.sem_inc(pool_settled, 1)
                for k in range(NT):
                    m = n * NT + k
                    nc.gpsimd.indirect_dma_start(
                        out=xg[:, :], out_offset=bass.IndirectOffsetOnAxis(ap=dest[c.par][:, m:m + 1], axis=0),
                        in_=xn2[c.par][:, k, :], in_offset=None).then_inc(scat_done[c.par], 16)

            def hidden(c, u):
                rows = HROWS[u]
                pool.wait_ge(hg_ready, c.index * UNITS + u + 2 + HEAD)
                pool.wait_ge(up_ready, c.index * UNITS + u + 2 + HEAD)
                block_ = hid[0:rows, hid_slot(c, u), :]
                nc.gpsimd.tensor_tensor(out=block_, in0=block_, in1=up[0:rows, (c.par + u) % 2, :], op=ALU.mult) \
                    .then_inc(h_ready, 1)

            class Body(Phases):
                eng = pool

                def start(self):
                    pool.sem_inc(h_ready, 1 + HEAD)
                    nc.gpsimd.memset(ident[:, :], 0.0).then_inc(pool_const, 1)
                    pool.wait_ge(pool_const, 1)
                    nc.gpsimd.affine_select(out=ident[:, :], in_=ident[:, :], compare_op=ALU.not_equal, fill=1.0,
                                            base=0, pattern=[[-1, P]], channel_multiplier=1).then_inc(pool_const, 1)
                    nc.gpsimd.memset(eps_col[:, :], STATE_EPS).then_inc(pool_const, 1)
                    nc.gpsimd.memset(xnT[:, :, 0:HALO], 0.0).then_inc(pool_const, 1)
                    nc.gpsimd.memset(mask[:, :], 0.0).then_inc(pool_const, 1)
                    nc.gpsimd.memset(zeros[:, :, :], 0.0).then_inc(pool_const, 1)
                    nc.gpsimd.memset(xn2[0][:, :, DM:ROW], 0.0)
                    nc.gpsimd.memset(xn2[1][:, :, DM:ROW], 0.0)
                    nc.gpsimd.memset(ones[:, :], 1.0).then_inc(pool_const, 1)
                    pool.wait_ge(pool_const, 7)
                    nc.gpsimd.affine_select(out=upper[:, :], in_=ones[:, :], compare_op=ALU.is_gt, fill=0.0,
                                            base=0, pattern=[[1, P]], channel_multiplier=-1).then_inc(pool_const, 1)
                    nc.gpsimd.iota(zeros[:, :, DM:DM + 1].bitcast(I32), pattern=[[P, NT]], base=TOK * PICKS,
                                   channel_multiplier=1)
                    nc.gpsimd.iota(home_i[:, :], pattern=[[P * PICKS, NT]], base=0, channel_multiplier=PICKS)
                    nc.gpsimd.iota(step_i[:, :], pattern=[[1, TILES]], base=0, channel_multiplier=0) \
                        .then_inc(pool_const, 1)
                    nc.gpsimd.iota(iota_i[:, :], pattern=[[1, EXPERTS]], base=0, channel_multiplier=0) \
                        .then_inc(pool_const, 1)
                    nc.gpsimd.memset(neg_half[:, :], -0.5).then_inc(pool_const, 1)
                    pool.wait_ge(pool_const, 11)
                    for i in range(2):
                        pool.dma_start(xg[EXPERTS * CAP + i * P:EXPERTS * CAP + (i + 1) * P, :], zeros[:, i, :]) \
                            .then_inc(scat_done[i], 16)
                    for n in range(2):
                        rstd(p_rstd, p_var, p_var_ready, p_rstd_ready, Chunk(0, n))
                    pool.wait_ge(dve_const, 4)
                    nc.gpsimd.partition_all_reduce(a_max[:, 1:2], a_max[:, 0:1], P, bass.bass_isa.ReduceOp.max) \
                        .then_inc(a_max_done, 1)
                    for n in range(MUL_LEAD):
                        b_times_dtu(Chunk(0, 0), n)

                def __call__(self, scan, post, proj, norm):
                    for slot in range(NS):
                        n = slot + MUL_LEAD
                        if scan and n < NS:
                            b_times_dtu(scan, n)
                        if scan and proj and n >= NS:
                            b_times_dtu(proj, n - NS)
                        if post and slot == 5:
                            rstd(o_rstd, o_var, o_var_ready, o_rstd_ready, post)
                        if norm and slot == 13:
                            rstd(p_rstd, p_var, p_var_ready, p_rstd_ready, norm)
                        if post:
                            for u in units_of(slot):
                                hidden(post, u)
                        if post and slot == 12:
                            scatter(post, 0)
                        if post and slot == 15:
                            scatter(post, 1)

                def tile(self, t, last):
                    hidden(counted(t), 0)
                    hidden(counted(t), 1)
                    if not (t.fixed() and t.index == 0):
                        self.send(t.plus(-1))
                    hidden(counted(t), 2)
                    if last:
                        self.send(t)

                def send(self, t):
                    pool.wait_ge(yt_ready, t.index + 1)
                    pool.wait_ge(ids_ready, t.index + 1)
                    if not (t.fixed() and t.index == 0):
                        last = t.plus(-1)
                        pool.wait_ge(sent[last.par], (last.pair + 1) * NT * 16)
                    pool.sem_inc(pool_settled, 1)
                    for k in range(NT):
                        nc.gpsimd.indirect_dma_start(
                            out=y_s[:, :], out_offset=bass.IndirectOffsetOnAxis(
                                ap=ids[t.par][:, k:k + 1], axis=0),
                            in_=yt[t.par][:, k, :], in_offset=None).then_inc(sent[t.par], 16)

                def combine(self, c):
                    pass

            run(Body())

        @block.vector
        def _(dve):
            vec_e = nc.vector

            def settle():
                dve.sem_inc(settled, 1)

            class Steps:

                def __init__(self, sem_, per, c):
                    self.sem, self.per, self.c, self.k = sem_, per, c, 0

                def did(self, ins):
                    self.k += 1
                    ins.then_inc(self.sem, 1)

                def sync(self):
                    dve.wait_ge(self.sem, self.c.index * self.per + self.k)

            def stats(c, src, st, mv, var, step, ready):
                for k in range(NT):
                    step.did(vec_e.bn_stats(st[:, k, :], src[:, k, :]))
                step.sync()
                settle()
                for k in range(NT):
                    step.did(vec_e.bn_aggr(mv[:, k, :], st[:, k, :]))
                step.sync()
                vec_e.tensor_scalar_add(var[:, :], mv[:, :, 1], LN_EPS).then_inc(ready, 1)

            def normed(dst, src, mv, rstd, ready):
                for k in range(NT):
                    vec_e.tensor_scalar(out=dst[:, k, 0:DM], in0=src[:, k, :], scalar1=mv[:, k, 0:1],
                                        scalar2=rstd[:, k:k + 1], op0=ALU.subtract, op1=ALU.mult).then_inc(ready, 1)

            def norm_stats(c):
                dve.wait_ge(x_loaded[c.par], c.pair * 16 + 16)
                stats(c, x_in[c.par], p_st, p_mv, p_var, Steps(norm_step, NORM_STEPS, c), p_var_ready)

            def norm_apply(c):
                dve.wait_ge(p_rstd_ready, c.index + 1)
                normed(x_in[c.par], x_in[c.par], p_mv, p_rstd, xn_ready)

            def proj_dt(c):
                dve.wait_ge(evac, c.index * EVACS + 5)
                d = dt[c.par][:, :, :]
                vec_e.tensor_scalar(out=d, in0=d, scalar1=DT_MIN, scalar2=DT_MAX, op0=ALU.max, op1=ALU.min) \
                    .then_inc(dt_ready, 1)
                dve.wait_ge(dt_ready, c.index + 1)
                vec_e.tensor_tensor(out=dtu[c.par][:, :, :], in0=d, in1=uT[:, :, :], op=ALU.mult) \
                    .then_inc(dtu_ready, 1)

            def proj_gate(c, k):
                dve.wait_ge(zt_ready, c.index * NT + k + 1)
                g = zs[c.par][:, k, :]
                vec_e.scalar_tensor_tensor(out=g, in0=g, scalar=1.0, in1=pr_bank[k][:, :], op0=ALU.add,
                                           op1=ALU.mult).then_inc(zs_done, 1)

            def scans(c, n, flag):
                with dve.If(flag > 0):
                    dve.wait_ge(da_ready, c.index * NS + n + 1)
                    vec_e.tensor_scalar_max(da[n % RING][:, :, :], da[n % RING][:, :, :], CLIP_EXP).then_inc(clip_done, 1)
                    dve.wait_ge(clip_done, c.index * NS + n + 1)
                    settle()
                dve.wait_ge(da_ready, c.index * NS + n + 1)
                if n == 0:
                    wait(dve, carry_done, c.index * NS)
                dve.wait_ge(v_ready, c.index * NS + n + 1)
                for b in range(KD):
                    init = 0.0 if c.fixed() and c.index == 0 else carry[:, n, b:b + 1]
                    s = v[n % RING][:, b, :]
                    last = vec_e.tensor_tensor_scan(s, da[n % RING][:, b, :], s, init, ALU.mult, ALU.add)
                last.then_inc(s_ready, 1)

            def keep_last(c, n):
                dve.wait_ge(s_ready, c.index * NS + n + 1)
                src = v[n % RING][:, :, TC - 1]
                if c.par:
                    if n == 0:
                        dve.wait_ge(mask_done, c.pair + 1)
                    vec_e.tensor_scalar(out=carry[:, n, :], in0=src, scalar1=mask[:, 0:1], scalar2=None,
                                        op0=ALU.mult).then_inc(carry_done, 1)
                else:
                    vec_e.tensor_copy(carry[:, n, :], src).then_inc(carry_done, 1)

            def c_times_state(c, n):
                for k in range(NT):
                    if n == 0:
                        dve.wait_ge(evac, c.index * EVACS + 8)
                    dve.wait_ge(tr_ready, c.index * NS * NT + NT * n + k + 1)
                    if n > 0:
                        dve.wait_ge(cmul_done, c.index * NS * NT + NT * (n - 1) + k + 1)
                    a = acc[c.par][:, k, :]
                    vec_e.scalar_tensor_tensor(out=a, in0=tr_bank[k][:, :], scalar=c_tok[c.par][:, k, n:n + 1],
                                               in1=a, op0=ALU.mult, op1=ALU.add).then_inc(cmul_done, 1)

            def post_gate(c):
                dve.wait_ge(cmul_done, (c.index + 1) * NS * NT)
                dve.wait_ge(zs_done, (c.index + 1) * NT)
                a = acc[c.par][:, :, :]
                vec_e.scalar_tensor_tensor(out=a, in0=a, scalar=0.5, in1=zs[c.par][:, :, :], op0=ALU.mult,
                                           op1=ALU.mult).then_inc(y_ready, 1)

            def finish(c, slot, step):
                if slot == 0:
                    post_gate(c)
                if slot == 5:
                    dve.wait_ge(o_ready, c.index * POST_USES + 3)
                    dve.wait_ge(res_loaded, c.index * 16 + 16)
                    dve.wait_ge(x1_stored[c.par], c.pair * 16 + 16)
                    r = x1[c.par][:, :, :].rearrange("p k d -> p (k d)")
                    step.did(vec_e.tensor_tensor(out=r, in0=o_bank[:, :], in1=x_res[:, :, :]
                                                 .rearrange("p k d -> p (k d)"), op=ALU.add))
                    step.sync()
                    dve.sem_inc(x1_ready, 1)
                    dve.sem_inc(o_free, 1)
                    stats(c, x1[c.par], o_st, o_mv, o_var, step, o_var_ready)
                if slot == 6:
                    dve.wait_ge(o_rstd_ready, c.index + 1)
                    dve.wait_ge(scat_done[c.par], c.pair * PICKS * NT * 16 + 16)
                    normed(xn2[c.par], x1[c.par], o_mv, o_rstd, xn2_ready)
                if slot == 9:
                    dve.wait_ge(o_ready, c.index * POST_USES + 5)
                    vec_e.tensor_copy(lg[:, :, :], o_bank[:, 0:NT * FFNS].rearrange("p (k e) -> p k e", k=NT)) \
                        .then_inc(o_free, 1)
                    dve.wait_ge(o_free, c.index * POST_USES + 5 + HEAD)
                    settle()
                    for k in range(NT):
                        step.did(vec_e.max(top[:, k, :], lg[:, k, 0:EXPERTS]))
                    step.sync()
                    vec_e.tensor_tensor(out=r_in[:, 0, :], in0=top[:, :, 1], in1=top[:, :, 0], op=ALU.subtract) \
                        .then_inc(r_in_ready, 1)
                    vec_e.tensor_scalar_mul(r_in[:, 1, :], lg[:, :, EXPERTS], -1.0).then_inc(r_in_ready, 1)
                    for k in range(NT):
                        step.did(vec_e.max_index(top_i[:, k, :], top[:, k, :], lg[:, k, 0:EXPERTS]))
                    step.sync()
                    step.did(vec_e.tensor_copy(top_f[:, :, :], top_i[:, :, 0:2]))
                    step.sync()
                    for k in range(NT):
                        for n in range(PICKS):
                            step.did(vec_e.tensor_scalar(out=hot[:, n, k, :], in0=iota_f[:, :],
                                                         scalar1=top_f[:, k, n:n + 1], scalar2=None,
                                                         op0=ALU.is_equal))
                    step.sync()
                    vec_e.tensor_tensor(out=sel[:, :, :], in0=hot[:, 0, :, :], in1=hot[:, 1, :, :], op=ALU.add) \
                        .then_inc(sel_ready, 1)
                if slot == 11:
                    dve.wait_ge(r_exp_ready, c.index + 1)
                    step.did(vec_e.tensor_scalar_add(r_den[:, :, :], r_exp[:, :, :], 1.0))
                    step.sync()
                    step.did(vec_e.reciprocal(r_w[:, :, :], r_den[:, :, :]))
                    step.sync()
                    step.did(vec_e.tensor_scalar_mul(r_w[:, :, :], r_w[:, :, :], 0.5))
                    step.sync()
                    step.did(vec_e.tensor_copy(w_sh[c.par][:, :], r_w[:, 1, :]))
                    vec_e.tensor_copy(w_all[:, c.index, 0:NT], r_w[:, 0, :])
                    vec_e.tensor_tensor(out=w_all[:, c.index, NT:2 * NT], in0=r_exp[:, 0, :], in1=r_w[:, 0, :],
                                        op=ALU.mult)
                if slot == 11:
                    dve.wait_ge(o_ready, c.index * POST_USES + 6)
                    for k in range(NT):
                        last = vec_e.tensor_tensor(out=row_of[:, k, :], in0=o_bank[:, k * EXPERTS:(k + 1) * EXPERTS],
                                                   in1=base[:, :], op=ALU.add)
                        step.did(last)
                    step.sync()
                    vec_e.tensor_tensor(out=base[:, :], in0=o_bank[:, NT * EXPERTS:(NT + 1) * EXPERTS],
                                        in1=base[:, :], op=ALU.add).then_inc(o_free, 1)
                    for n in range(PICKS):
                        last = vec_e.tensor_tensor(out=picked[:, n, :, :], in0=hot[:, n, :, :], in1=row_of[:, :, :],
                                                   op=ALU.mult)
                    step.did(last)
                    step.sync()
                    step.did(vec_e.tensor_reduce(dest_f[:, :], picked[:, :, :, :]
                                                 .rearrange("p n k e -> p (n k) e"), AX.X, ALU.add))
                    step.sync()
                    vec_e.tensor_copy(xn2[c.par][:, :, DM].bitcast(U32), home[:, :])
                    vec_e.tensor_copy(dest[c.par][:, :], dest_f[:, :]).then_inc(dest_ready, 1)
                if slot == 15:
                    dve.wait_ge(scat_done[c.par], c.pair * PICKS * NT * 16 + 16 + NT * 16)
                    step.did(vec_e.tensor_scalar_add(home[:, :], home[:, :], 1.0))
                    step.sync()
                    vec_e.tensor_copy(xn2[c.par][:, :, DM].bitcast(U32), home[:, :]).then_inc(dest_ready, 1)
                    dve.wait_ge(dest_ready, c.index * 2 + 2)
                    step.did(vec_e.tensor_scalar_add(home[:, :], home[:, :], float(TC * PICKS - 1)))
                    assert step.k == POST_STEPS, step.k

            def gated(c, u):
                rows = HROWS[u]
                dve.wait_ge(th_ready, c.index * UNITS + u + 1)
                dve.wait_ge(up_ready, c.index * UNITS + u + 2 + HEAD)
                h = hid[0:rows, hid_slot(c, u), :]
                vec_e.scalar_tensor_tensor(out=h, in0=h, scalar=1.0, in1=gu_bank[(c.par + u) % 2][0:rows, 0:TC],
                                           op0=ALU.add, op1=ALU.mult).then_inc(hg_ready, 1)

            def mix(c):
                dve.wait_ge(dn_ready, c.index + 2 + HEAD)
                for k in range(NT):
                    r = x1[c.par][:, k, :]
                    last = vec_e.scalar_tensor_tensor(out=r, in0=dn_bank[:, k * DM:(k + 1) * DM],
                                                      scalar=w_sh[c.par][:, k:k + 1], in1=r, op0=ALU.mult,
                                                      op1=ALU.add)
                last.then_inc(mix_done, 1)

            def tile_table():
                done = [0]

                def did(ins):
                    done[0] += 1
                    ins.then_inc(table_step, 1)
                    dve.wait_ge(table_step, done[0])

                full = [P, TILES, EXPERTS]
                did(vec_e.tensor_copy(tab_zero[:, :], base[:, :]))
                did(vec_e.tensor_tensor(out=n_tok[:, :], in0=base[:, :], in1=first_row[:, :], op=ALU.subtract))
                did(vec_e.tensor_scalar_mul(t_row[:, :], step_f[:, :], float(TILE)))
                did(vec_e.tensor_tensor(
                    out=n_gt[:, :, :], in0=n_tok[:, :].unsqueeze(2).to_broadcast([P, EXPERTS, TOK // TILE]),
                    in1=t_row[:, 0:TOK // TILE].unsqueeze(1).to_broadcast([P, EXPERTS, TOK // TILE]), op=ALU.is_gt))
                did(vec_e.tensor_reduce(n_tiles[:, :], n_gt[:, :, :], AX.X, ALU.add))
                did(vec_e.tensor_tensor_scan(n_incl[:, :], ones[:, 0:EXPERTS], n_tiles[:, :], 0.0, ALU.mult, ALU.add))
                did(vec_e.tensor_tensor(out=past[:, :, :], in0=n_incl[:, :].unsqueeze(1).to_broadcast(full),
                                        in1=step_f[:, :].unsqueeze(2).to_broadcast(full), op=ALU.is_le))
                did(vec_e.tensor_reduce(t_exp[:, :], past[:, :, :], AX.X, ALU.add))
                did(vec_e.tensor_tensor(out=past_t[:, :, :], in0=past[:, :, :],
                                        in1=n_tiles[:, :].unsqueeze(1).to_broadcast(full), op=ALU.mult))
                did(vec_e.tensor_reduce(t_used[:, :], past_t[:, :, :], AX.X, ALU.add))
                did(vec_e.tensor_tensor(out=t_row[:, :], in0=step_f[:, :], in1=t_used[:, :], op=ALU.subtract))
                did(vec_e.tensor_scalar_mul(t_row[:, :], t_row[:, :], float(TILE)))
                did(vec_e.tensor_scalar_mul(t_used[:, :], t_exp[:, :], float(CAP)))
                did(vec_e.tensor_tensor(out=t_row[:, :], in0=t_row[:, :], in1=t_used[:, :], op=ALU.add))
                did(vec_e.tensor_copy(tab[:, 0, :], t_exp[:, :]))
                did(vec_e.tensor_scalar_min(t_row[:, :], t_row[:, :], float(EXPERTS * CAP)))
                vec_e.tensor_copy(tab[:, 1, :], t_row[:, :]).then_inc(tab_ready, 1)

            class Body(Phases):
                eng = dve

                def start(self):
                    dve.sem_inc(hg_ready, 1 + HEAD)
                    dve.sem_inc(o_free, HEAD)
                    dve.sem_inc(mix_done, HEAD)
                    dve.wait_ge(w_early, 16 * EARLY_LOADS)
                    dve.wait_ge(pool_const, 11)
                    for b in range(KD):
                        last = vec_e.tensor_scalar(out=diag_d[:, b, :], in0=ident[:, :], scalar1=vec[:, 2, b:b + 1],
                                                   scalar2=None, op0=ALU.mult)
                    last.then_inc(dve_const, 1)
                    vec_e.tensor_copy(step_f[:, :], step_i[:, :])
                    vec_e.tensor_copy(home[:, :], home_i[:, :])
                    vec_e.tensor_copy(iota_f[:, :], iota_i[:, :]).then_inc(dve_const, 1)
                    dve.wait_ge(dve_const, 2)
                    vec_e.tensor_scalar_mul(first_row[:, :], iota_f[:, :], float(CAP))
                    vec_e.tensor_scalar_mul(base[:, :], iota_f[:, :], float(CAP))
                    dve.wait_ge(a_exp_done, 1)
                    vec_e.tensor_scalar_mul(neg_a[:, :, :], a_exp[:, :, :], -1.0).then_inc(dve_const, 1)
                    vec_e.reduce_max(a_max[:, 0:1], a_exp[:, :, :].rearrange("p b n -> p (b n)"), AX.X) \
                        .then_inc(dve_const, 1)
                    for n in range(2):
                        norm_stats(Chunk(0, n))
                        norm_apply(Chunk(0, n))
                    dve.wait_ge(a_max_done, 1)
                    vec_e.tensor_scalar(out=a_flag[:, :], in0=a_max[:, 1:2], scalar1=CLIP, scalar2=None,
                                        op0=ALU.is_gt).then_inc(dve_const, 1)
                    dve.wait_ge(dve_const, 5)
                    self.flag = dve.value_load(a_flag[0:1, 0:1], min_val=0, max_val=1)
                    proj_dt(Chunk(0, 0))
                    proj_gate(Chunk(0, 0), 0)
                    proj_gate(Chunk(0, 0), 1)

                def __call__(self, scan, post, proj, norm):
                    step = Steps(post_step, POST_STEPS, post) if post else None
                    for slot in range(NS):
                        if slot == 0 and scan and not scan.par:
                            vec_e.tensor_scalar(out=mask[:, :], in0=mask[:, :], scalar1=-1.0, scalar2=1.0,
                                                op0=ALU.mult, op1=ALU.add).then_inc(mask_done, 1)
                        if scan:
                            scans(scan, slot, self.flag)
                        if slot == 0 and post:
                            c_times_state(post, NS - 1)
                        if slot > 0 and scan:
                            c_times_state(scan, slot - 1)
                        if scan:
                            keep_last(scan, slot)
                        if post:
                            finish(post, slot, step)
                        if proj and slot == 8:
                            proj_dt(proj)
                        if proj and slot in (10, 11):
                            proj_gate(proj, slot - 10)
                        if norm and slot == 13:
                            norm_stats(norm)
                        if norm and slot == 14:
                            norm_apply(norm)
                        if post:
                            for u in units_of(slot):
                                gated(post, u)
                            if slot == MIX_SLOT:
                                mix(post)

                def before_tiles(self):
                    tile_table()

                def tile(self, t, last):
                    dve.wait_ge(xt_loaded[t.par], t.pair * 16 + 16)
                    if not (t.fixed() and t.pair == 0):
                        dve.wait_ge(sent[t.par], t.pair * NT * 16)
                    vec_e.tensor_copy(ids[t.par][:, :], xt[t.par][:, :, DM].bitcast(U32)).then_inc(ids_ready, 1)
                    for u in range(UNITS):
                        gated(counted(t), u)

                def combine(self, c):
                    vec_e.tensor_copy(w_now[c.par][:, :], w_all[:, c.index, :]).then_inc(w_ready, 1)
                    dve.wait_ge(w_ready, c.index + 1)
                    dve.wait_ge(x1_loaded[c.par], c.pair * 16 + 16)
                    dve.wait_ge(pick_loaded[c.par], c.pair * 16 + 16)
                    for n in range(PICKS):
                        if n:
                            dve.wait_ge(pick_step, c.index + 1)
                        for k in range(NT):
                            m = n * NT + k
                            r = x1[c.par][:, k, :]
                            last = vec_e.scalar_tensor_tensor(out=r, in0=pick[c.par][:, k, n * DM:(n + 1) * DM],
                                                              scalar=w_now[c.par][:, m:m + 1], in1=r, op0=ALU.mult,
                                                              op1=ALU.add)
                        last.then_inc(pick_step if n == 0 else combined, 1)

            assert PER_SEQ == 4
            run(Body())


def kernel(**inputs):
    import numpy as np
    import concourse.bacc as bacc
    from concourse import mybir as _mybir
    from concourse.bass_utils import run_bass_kernel_spmd

    g = {k: np.asarray(v) for k, v in inputs.items()}
    cont = np.ascontiguousarray

    def rows(a):
        return cont(a.reshape(-1, P, a.shape[1]).transpose(1, 0, 2))

    def cols(a):
        return cont(np.moveaxis(a.reshape(-1, P, *a.shape[1:]), 0, 1))

    in_w = g["L0_attn_in_proj_w"]
    gu = np.concatenate([np.concatenate([g["L0_ffn_w_gate"], g["L0_ffn_w_up"]], axis=2),
                         np.concatenate([g["L0_ffn_sw_gate"], g["L0_ffn_sw_up"]], axis=1)[None]], axis=0)
    dn = np.concatenate([g["L0_ffn_w_down"], g["L0_ffn_sw_down"][None]], axis=0)
    dn = np.concatenate([dn, np.zeros((FFNS, HB * P - HID, DM), dn.dtype)], axis=1)
    arrays = {
        "x": cont(g["L0_attn_x"].reshape(TOK, DM)),
        "wx": rows(in_w[0:DI]),
        "wconv": cont(g["L0_attn_conv_w"].transpose(1, 2, 0).reshape(KD, P, TAPS, DI).transpose(1, 0, 2, 3)),
        "wz": rows(in_w[DI:2 * DI].T),
        "wdt": rows(g["L0_attn_dt_w"].T),
        "wbc": rows(np.concatenate([g["L0_attn_B_w"], g["L0_attn_C_w"]], axis=0).T),
        "wout": rows(g["L0_attn_out_w"].T),
        "conv_b": cols(g["L0_attn_conv_b"]),
        "dt_b": cols(g["L0_attn_dt_b"]),
        "d_skip": cols(g["L0_attn_D"]),
        "a_log": cols(g["L0_attn_A_log"]),
        "wgate": rows(np.concatenate([g["L0_ffn_gate_w"], g["L0_ffn_shared_gate_w"]], axis=0).T),
        "wgu": cont(gu.reshape(FFNS, KM, P, 2 * HID).transpose(0, 2, 1, 3)),
        "wd": cont(dn.reshape(FFNS, HB, P, DM).transpose(0, 2, 1, 3)),
    }
    nc = bacc.Bacc("TRN2", target_bir_lowering=False, num_devices=1)
    args = [nc.dram_tensor(f"in_{k}", a.shape, _mybir.dt.from_np(a.dtype), kind="ExternalInput").ap()
            for k, a in arrays.items()]
    out = nc.dram_tensor("out_0", (TOK, DM), F32, kind="ExternalOutput").ap()
    build(nc, *args, out)
    r = run_bass_kernel_spmd(nc, [{f"in_{k}": a for k, a in arrays.items()}], core_ids=[0])
    return r.results[0]["out_0"].reshape(BATCH, SEQ, DM)
```

```python
from contextlib import ExitStack

import concourse.bass as bass
from concourse import mybir

F32 = mybir.dt.float32
F32R = mybir.dt.float32r
I32 = mybir.dt.int32
U32 = mybir.dt.uint32
ALU = mybir.AluOpType
ACT = mybir.ActivationFunctionType
AX = mybir.AxisListType

BATCH, SEQ, DM = 8, 1024, 256
DI, NS, TAPS = 512, 16, 4
EXPERTS, HID = 8, 352
TOK = BATCH * SEQ
P = 128
TC = 256
CHUNKS = TOK // TC
PER_SEQ = SEQ // TC
NT = TC // P
KM = DM // P
KD = DI // P
FFNS = EXPERTS + 1
HB = 3
HROWS = [P, P, HID - 2 * P]
UNITS = HB
PICKS = 2
TILE = TC
CAP = TOK + TILE
TILES = TOK * PICKS // TILE + EXPERTS
XG_ROWS = EXPERTS * CAP + TILE
OUT_ROWS = TOK + TILE
HALO = TAPS - 1
NEAR = 4
PIECES = NS // NEAR
THRING = 2 * HB
RING = 4
MUL_LEAD, DECAY_LEAD = 3, 2
PASSES = [(0, 0), (0, 1), (1, 0)]
AIDED = range(12, 14)
ROW = DM + 4
ID_COL, W_COL = DM, DM + 1
LN_EPS, STATE_EPS, DT_MIN, DT_MAX, CLIP = 1e-5, 1e-6, 1e-4, 1.0, 5.0
CLIP_EXP = 0.006737946999085467

EVACS, PROJ_USES, POST_USES = 8, 10, 6
HEAD = 1


class Chunk:

    def __init__(self, pair, par):
        self.pair, self.par = pair, par
        self.index = pair * 2 + par

    def plus(self, n):
        k = self.par + n
        return Chunk(self.pair + k // 2, k % 2)

    def fixed(self):
        return isinstance(self.index, int)


def wait(eng, sem, value):
    if not isinstance(value, int) or value > 0:
        eng.wait_ge(sem, value)


UNIT_SLOT = [9, 10, 11]
DOWN_SLOT, MIX_SLOT = 13, 14


def units_of(slot):
    return [u for u in range(UNITS) if UNIT_SLOT[u] == slot]


def build(nc, x, wx, wconv, wz, wdt, wbc, wout, conv_b, dt_b, d_skip, a_log, wgate, wgu, wd, out):
    x_v = x.rearrange("(c k p) d -> c p k d", p=P, k=NT)
    out_v = out[0:TOK, :].rearrange("(c k p) d -> c p k d", p=P, k=NT)
    xg = nc.dram_tensor("x_by_expert", [XG_ROWS, ROW], F32, kind="Internal").ap()
    b_scratch = nc.dram_tensor("b_scratch", [2, NS, TC], F32, kind="Internal").ap()

    ctx = ExitStack()
    with ctx:
        def sb(name, shape, dt=F32):
            return ctx.enter_context(nc.sbuf_tensor(name, shape, dt))

        def sem(name):
            return ctx.enter_context(nc.semaphore(name))

        w_gu = sb("w_gu", [P, KM, 2 * HID])
        w_dn = sb("w_dn", [P, HB, DM])
        w_conv = [sb(f"w_conv{i}", [P, TAPS, KM, DI], F32R) for i in range(2)]
        w_z = [sb(f"w_z{i}", [P, KM, DI], F32R) for i in range(2)]
        w_dt = sb("w_dt", [P, KD, DI])
        w_bc = sb("w_bc", [P, KD, 2 * NS])
        w_out = sb("w_out", [P, KD, DM])
        w_rt = sb("w_rt", [P, KM, FFNS])
        ident = sb("ident", [P, P])
        diag_d = sb("diag_d", [P, KD, P])
        vec = sb("vec", [P, 3, KD])
        a_raw = sb("a_raw", [P, KD, NS])
        a_exp = sb("a_exp", [P, KD, NS])
        neg_a = sb("neg_a", [P, KD, NS])
        a_max = sb("a_max", [P, 2])
        a_flag = sb("a_flag", [P, 1], I32)
        upper = sb("upper", [P, P])
        ones = sb("ones", [P, P])
        zeros = sb("zeros", [P, NT, ROW])
        step_i = sb("step_i", [P, TILES], I32)
        step_f = sb("step_f", [P, TILES])
        eps_col = sb("eps_col", [P, 1])
        neg_half = sb("neg_half", [P, NT])
        iota_i = sb("iota_i", [P, EXPERTS], I32)
        iota_f = sb("iota_f", [P, EXPERTS])
        halo_zero = sb("halo_zero", [P, KM, HALO])
        mask = sb("mask", [P, 1])

        x_in = [sb(f"x_in{i}", [P, NT, DM]) for i in range(2)]
        p_st = sb("p_st", [P, NT, 6])
        p_mv = sb("p_mv", [P, NT, 2])
        p_var = sb("p_var", [P, NT])
        p_rstd = sb("p_rstd", [P, NT])
        xnT = [sb(f"xnT{i}", [P, KM, HALO + TC], F32R) for i in range(2)]
        uT = sb("uT", [P, KD, TC])
        b_row = sb("b_row", [NS, TC])
        dtu = [sb(f"dtu{i}", [P, KD, TC]) for i in range(2)]
        zs = [sb(f"zs{i}", [P, NT, DI]) for i in range(2)]
        c_tok = [sb(f"c_tok{i}", [P, NT, NS]) for i in range(2)]
        acc = [sb(f"acc{i}", [P, NT, DI]) for i in range(2)]
        b_all = [sb(f"b_all{i}", [P, NEAR, TC]) for i in range(2)]
        room = sb("room", [P, 2 * RING + 2, KD, TC])
        v = [room[:, i, :, :] for i in range(RING)]
        da = [room[:, RING + i, :, :] for i in range(RING)]
        dt = [room[:, 2 * RING + i, :, :] for i in range(2)]
        aid = [sb(f"aid{i}", [P, DI]) for i in range(2)]
        carry = sb("carry", [P, NS, KD])
        yT = sb("yT", [P, KD, TC])
        x_res = sb("x_res", [P, NT, DM])
        x1 = [sb(f"x1_{i}", [P, NT, DM]) for i in range(2)]
        o_st = sb("o_st", [P, NT, 6])
        o_mv = sb("o_mv", [P, NT, 2])
        o_var = sb("o_var", [P, NT])
        o_rstd = sb("o_rstd", [P, NT])
        xn2 = [sb(f"xn2_{i}", [P, NT, ROW]) for i in range(2)]
        xn2T = sb("xn2T", [P, KM, TC])
        lg = sb("lg", [P, NT, FFNS])
        top = sb("top", [P, NT, 8])
        top_i = sb("top_i", [P, NT, 8], U32)
        top_f = sb("top_f", [P, NT, 2])
        r_in = sb("r_in", [P, 2, NT])
        r_exp = sb("r_exp", [P, 2, NT])
        r_den = sb("r_den", [P, 2, NT])
        r_w = sb("r_w", [P, 2, NT])
        w_sh = [sb(f"w_sh{i}", [P, NT]) for i in range(2)]
        w_second = [sb(f"w_second{i}", [P, NT]) for i in range(2)]
        hot = sb("hot", [P, PICKS, NT, EXPERTS])
        sel = sb("sel", [P, NT, EXPERTS])
        row_of = sb("row_of", [P, NT, EXPERTS])
        picked = sb("picked", [P, PICKS, NT, EXPERTS])
        dest_f = sb("dest_f", [P, PICKS * NT])
        dest = [sb(f"dest{i}", [P, PICKS * NT], U32) for i in range(2)]
        token_i = sb("token_i", [P, NT], I32)
        token_f = sb("token_f", [P, NT])
        base = sb("base", [P, EXPERTS])
        first_row = sb("first_row", [P, EXPERTS])
        n_tok = sb("n_tok", [P, EXPERTS])
        n_gt = sb("n_gt", [P, EXPERTS, TOK // TILE])
        n_tiles = sb("n_tiles", [P, EXPERTS])
        n_incl = sb("n_incl", [P, EXPERTS])
        past = sb("past", [P, TILES, EXPERTS])
        past_t = sb("past_t", [P, TILES, EXPERTS])
        t_exp = sb("t_exp", [P, TILES])
        t_used = sb("t_used", [P, TILES])
        t_row = sb("t_row", [P, TILES])
        tab = sb("tab", [P, 2, TILES], I32)
        tab_zero = sb("tab_zero", [P, EXPERTS], I32)
        parts = [("t_gu", KM, 2 * HID), ("t_dn", HB, DM), ("xt", NT, ROW), ("xtT", KM, TILE), ("yt", NT, DM)]
        assert max(2 * sum(k * n for _, k, n in parts), KD * (TAPS * DI + DM) + KM * DI) <= (2 * RING + 2) * KD * TC
        late = room[:, :, :, :].rearrange("p r b t -> p (r b t)")
        views, at = {}, 0
        for name, k, n in parts:
            views[name] = []
            for _ in range(2):
                views[name].append(late[:, at:at + k * n].rearrange("p (k n) -> p k n", k=k))
                at += k * n
        t_gu, t_dn, xt, xtT, yt = (views[name] for name, _, _ in parts)
        raw_z = late[:, KD * (TAPS * DI + DM):KD * (TAPS * DI + DM) + KM * DI].rearrange("p (k i) -> p k i", k=KM)
        raw_conv = late[:, 0:KD * TAPS * DI].rearrange("p (m t j) -> p m t j", m=KD, t=TAPS)
        raw_x = late[:, KD * TAPS * DI:KD * (TAPS * DI + DM)].rearrange("p (m i) -> p m i", m=KD)
        ids = [sb(f"ids{i}", [P, NT], U32) for i in range(2)]
        wts = [sb(f"wts{i}", [P, NT]) for i in range(2)]
        hid = sb("hid", [P, THRING, TC])
        up = sb("up", [P, 2, TC])

        banks = [ctx.enter_context(nc.psum_tensor(f"bank{i}", [P, 512], F32)) for i in range(8)]
        tr_bank, gu_bank, pr_bank, o_bank, dn_bank = banks[0:2], banks[2:4], banks[4:6], banks[6], banks[7]

        w_early = sem("w_early")
        w_raw = sem("w_raw")
        pool_const = sem("pool_const")
        dve_const = sem("dve_const")
        a_exp_done = sem("a_exp_done")
        a_max_done = sem("a_max_done")
        comp_mm = sem("comp_mm")
        comp_done = sem("comp_done")
        low_done = sem("low_done")
        x_loaded = [sem(f"x_loaded{i}") for i in range(2)]
        res_loaded = sem("res_loaded")
        b_written = sem("b_written")
        b_loaded = [sem(f"b_loaded{i}") for i in range(2)]
        mask_done = sem("mask_done")
        norm_step = sem("norm_step")
        p_var_ready = sem("p_var_ready")
        p_rstd_ready = sem("p_rstd_ready")
        xn_ready = sem("xn_ready")
        pr_ready = sem("pr_ready")
        halo_done = sem("halo_done")
        halo_low = sem("halo_low")
        xn_low = sem("xn_low")
        evac = sem("evac")
        b_ready = sem("b_ready")
        zt_ready = sem("zt_ready")
        zs_done = sem("zs_done")
        dt_ready = sem("dt_ready")
        dtu_ready = sem("dtu_ready")
        da_ready = sem("da_ready")
        v_mul = sem("v_mul")
        v_ready = sem("v_ready")
        clip_done = sem("clip_done")
        s_ready = sem("s_ready")
        carry_done = sem("carry_done")
        tr_ready = sem("tr_ready")
        taken = [sem(f"taken{i}") for i in range(NT)]
        aid_ready = sem("aid_ready")
        aid_added = sem("aid_added")
        y_ready = sem("y_ready")
        o_ready = sem("o_ready")
        o_free = sem("o_free")
        x1_ready = sem("x1_ready")
        post_step = sem("post_step")
        o_var_ready = sem("o_var_ready")
        o_rstd_ready = sem("o_rstd_ready")
        xn2_ready = sem("xn2_ready")
        r_in_ready = sem("r_in_ready")
        r_exp_ready = sem("r_exp_ready")
        sel_ready = sem("sel_ready")
        dest_ready = sem("dest_ready")
        scat_done = [sem(f"scat_done{i}") for i in range(2)]
        x1_stored = [sem(f"x1_stored{i}") for i in range(2)]
        table_step = sem("table_step")
        tab_ready = sem("tab_ready")
        zero_done = sem("zero_done")
        xt_loaded = [sem(f"xt_loaded{i}") for i in range(2)]
        gu_loaded = [sem(f"gu_loaded{i}") for i in range(2)]
        dn_loaded = [sem(f"dn_loaded{i}") for i in range(2)]
        ids_ready = sem("ids_ready")
        yt_ready = sem("yt_ready")
        sent = [sem(f"sent{i}") for i in range(2)]
        dump_zero = sem("dump_zero")
        gu_ready = sem("gu_ready")
        th_ready = sem("th_ready")
        up_ready = sem("up_ready")
        hg_ready = sem("hg_ready")
        h_ready = sem("h_ready")
        dn_ready = sem("dn_ready")
        mix_done = sem("mix_done")
        settled = sem("settled")
        pool_settled = sem("pool_settled")
        sp_settled = sem("sp_settled")

        NORM_STEPS = 2 * NT
        POST_STEPS = 1 + 2 * NT + (2 * NT + 1 + PICKS * NT) + 5 + (NT + 2) + 1
        EARLY_LOADS, RAW_LOADS = 11, 2

        def hid_slot(c, u):
            return (u + c.par * UNITS) % THRING

        def run(body):
            body.start()
            c0 = Chunk(0, 0)
            body(c0, None, c0.plus(1), c0.plus(2))
            with body.eng.Fori(0, (CHUNKS - 4) // 2) as i:
                for c in (Chunk(i, 1), Chunk(i, 1).plus(1)):
                    body(c, c.plus(-1), c.plus(1), c.plus(2))
            for n in range(CHUNKS - 3, CHUNKS + 1):
                c = Chunk(n // 2, n % 2)
                body(c if n < CHUNKS else None, c.plus(-1), c.plus(1) if n + 1 < CHUNKS else None,
                     c.plus(2) if n + 2 < CHUNKS else None)
            body.before_tiles()
            for par in range(2):
                body.tile(Chunk(0, par), False)
            with body.eng.Fori(1, TILES // 2 - 1) as i:
                for par in range(2):
                    body.tile(Chunk(i, par), False)
            for par in range(2):
                body.tile(Chunk(TILES // 2 - 1, par), par == 1)

        def counted(t):
            return Chunk(t.pair + CHUNKS // 2, t.par)

        class Phases:
            def before_tiles(self):
                pass

        block = ctx.enter_context(nc.Block())

        @block.sync
        def _(sp):
            def sp_wait(sem_, value):
                wait(sp, sem_, value)
                sp.sem_inc(sp_settled, 1)

            def load_x(c):
                sp_wait(pr_ready, c.plus(-2).index * PROJ_USES + 1)
                sp.dma_start(x_in[c.par][:, :, :], x_v[c.index, :, :, :]).then_inc(x_loaded[c.par], 16)

            def load_res(c):
                sp_wait(x1_ready, c.index)
                sp.dma_start(x_res[:, :, :], x_v[c.index, :, :, :]).then_inc(res_loaded, 16)

            def write_b(c):
                sp_wait(b_ready, c.index + 1)
                sp_wait(b_loaded[0], c.plus(-1).index * 32)
                sp_wait(b_loaded[1], c.plus(-1).index * 32)
                sp.dma_start(b_scratch[c.par, :, :], b_row[:, :]).then_inc(b_written, 16)

            def load_b(c, p):
                sp_wait(b_written, c.index * 16 + 16)
                sp_wait(v_mul, c.index * NS + NEAR * (p - 1))
                src = b_scratch[c.par, NEAR * p:NEAR * (p + 1), :].rearrange("n t -> (n t)") \
                    .partition_broadcast(P)
                sp.dma_start(b_all[p % 2][:, :, :].rearrange("p n t -> p (n t)"), src) \
                  .then_inc(b_loaded[p % 2], 16)

            def store(c):
                sp_wait(mix_done, c.index + 1 + HEAD)
                sp.dma_start(out_v[c.index, :, :, :], x1[c.par][:, :, :]).then_inc(x1_stored[c.par], 16)

            class Body(Phases):
                eng = sp

                def start(self):
                    for i in range(2):
                        sp.sem_inc(x1_stored[i], 16)
                    load_x(Chunk(0, 0))
                    load_x(Chunk(0, 1))
                    sp.dma_start(raw_x, wx).then_inc(w_raw, 16)
                    sp.dma_start(raw_conv, wconv).then_inc(w_raw, 16)
                    sp.dma_start(vec[:, 0, :], conv_b).then_inc(w_early, 16)
                    sp.dma_start(vec[:, 1, :], dt_b).then_inc(w_early, 16)
                    sp.dma_start(vec[:, 2, :], d_skip).then_inc(w_early, 16)
                    sp.dma_start(a_raw[:, :, :], a_log).then_inc(w_early, 16)
                    sp.dma_start(w_dt[:, :, :], wdt).then_inc(w_early, 16)
                    sp.dma_start(w_bc[:, :, :], wbc).then_inc(w_early, 16)
                    sp.dma_start(raw_z, wz).then_inc(w_early, 16)
                    sp.dma_start(w_out[:, :, :], wout).then_inc(w_early, 16)
                    sp.dma_start(w_rt[:, :, :], wgate).then_inc(w_early, 16)
                    sp.dma_start(w_gu[:, :, :], wgu[EXPERTS, :, :, :]).then_inc(w_early, 16)
                    sp.dma_start(w_dn[:, :, :], wd[EXPERTS, :, :, :]).then_inc(w_early, 16)
                    write_b(Chunk(0, 0))
                    load_b(Chunk(0, 0), 0)
                    load_b(Chunk(0, 0), 1)

                def __call__(self, scan, post, proj, norm):
                    if norm:
                        load_x(norm)
                    if scan:
                        load_b(scan, 2)
                        load_res(scan)
                        load_b(scan, 3)
                    if proj:
                        write_b(proj)
                        load_b(proj, 0)
                        load_b(proj, 1)
                    if post:
                        store(post)

                def before_tiles(self):
                    sp.wait_ge(tab_ready, 1)
                    for e in range(EXPERTS):
                        row = sp.value_load(tab_zero[0:1, e:e + 1], min_val=0, max_val=XG_ROWS - TILE)
                        sp.dma_start(xg_rows(row), zeros[:, :, :]).then_inc(zero_done, 16)
                    sp.wait_ge(zero_done, 16 * EXPERTS)
                    for i in range(2):
                        sp.wait_ge(scat_done[i], CHUNKS // 2 * PICKS * NT * 16 + 16)

                    self.load_tokens(Chunk(0, 0))

                def load_tokens(self, t):
                    row = sp.value_load(tab[0:1, 1, bass.ds(t.index, 1)], min_val=0, max_val=XG_ROWS - TILE)
                    sp_wait(o_ready, POST_USES * CHUNKS + t.index - 1)
                    sp_wait(ids_ready, t.index - 1)
                    sp.dma_start(xt[t.par], xg_rows(row)).then_inc(xt_loaded[t.par], 16)

                def tile(self, t, last):
                    e = sp.value_load(tab[0:1, 0, bass.ds(t.index, 1)], min_val=0, max_val=EXPERTS)
                    sp_wait(gu_ready, (counted(t).index - 1) * UNITS)
                    sp.dma_start(t_gu[t.par], wgu[bass.ds(e, 1), :, :, :].rearrange("a p k n -> (a p) k n")) \
                      .then_inc(gu_loaded[t.par], 16)
                    if not last:
                        self.load_tokens(t.plus(1))
                    sp_wait(dn_ready, counted(t).index + HEAD)
                    sp.dma_start(t_dn[t.par], wd[bass.ds(e, 1), :, :, :].rearrange("a p k n -> (a p) k n")) \
                      .then_inc(dn_loaded[t.par], 16)

            def xg_rows(row):
                return xg[bass.ds(row, TILE), :].rearrange("(k p) d -> p k d", p=P)

            run(Body())
            for i in range(2):
                sp.wait_ge(sent[i], 16 * NT * (TILES // 2))

        @block.tensor
        def _(pe):
            mm = nc.tensor.matmul

            def transposes(bank, tiles):
                for n, tile in enumerate(tiles):
                    last = nc.tensor.transpose(bank[:, n * P:(n + 1) * P], tile, ident[:, :])
                return last

            def proj_norm(c):
                pe.wait_ge(xn_ready, c.index * NT + NT)
                wait(pe, evac, c.index * EVACS - 1)
                transposes(pr_bank[0], [x_in[c.par][:, k, b * P:(b + 1) * P] for b in range(KM) for k in range(NT)]) \
                    .then_inc(pr_ready, 1)

            def proj_conv(c, half, j):
                pe.wait_ge(evac, c.index * EVACS + 1)
                col = (2 * half + j) * P
                for x_part, w_part in PASSES:
                    if x_part:
                        pe.wait_ge(xn_low, c.index + 1)
                    for n, (t, b) in enumerate((t, b) for t in range(TAPS) for b in range(KM)):
                        last = mm(pr_bank[1 - half][:, j * TC:(j + 1) * TC], w_conv[w_part][:, t, b, col:col + P],
                                  xnT[x_part][:, b, t:t + TC], start=(n == 0 and (x_part, w_part) == PASSES[0]),
                                  stop=(n == TAPS * KM - 1 and (x_part, w_part) == PASSES[-1]))
                if j == 1:
                    last.then_inc(pr_ready, 1)

            def proj_dt(c, half):
                pe.wait_ge(evac, c.index * EVACS + 3)
                for j in range(2):
                    col = (2 * half + j) * P
                    for b in range(KD):
                        last = mm(pr_bank[1 - half][:, j * TC:(j + 1) * TC], w_dt[:, b, col:col + P],
                                  uT[:, b, :], start=(b == 0), stop=(b == KD - 1))
                last.then_inc(pr_ready, 1)

            def proj_bc(c):
                pe.wait_ge(evac, c.index * EVACS + 4)
                for b in range(KD):
                    mm(pr_bank[1][0:NS, 0:TC], w_bc[:, b, 0:NS], uT[:, b, :], start=(b == 0), stop=(b == KD - 1))
                for k in range(NT):
                    for b in range(KD):
                        last = mm(pr_bank[1][:, TC + k * NS:TC + (k + 1) * NS], uT[:, b, k * P:(k + 1) * P],
                                  w_bc[:, b, NS:2 * NS], start=(b == 0), stop=(b == KD - 1))
                last.then_inc(pr_ready, 1)

            def proj_z(c, k):
                pe.wait_ge(evac, c.index * EVACS + 5 + k)
                for n, (b, (x_part, w_part)) in enumerate((b, q) for b in range(KM) for q in PASSES):
                    last = mm(pr_bank[k][:, :], xnT[x_part][:, b, HALO + k * P:HALO + (k + 1) * P],
                              w_z[w_part][:, b, :], start=(n == 0), stop=(n == KM * len(PASSES) - 1))
                last.then_inc(pr_ready, 1)

            def proj_skip(c, k):
                pe.wait_ge(zs_done, c.index * NT + k + 1)
                for b in range(KD):
                    last = mm(pr_bank[k][:, b * P:(b + 1) * P], uT[:, b, k * P:(k + 1) * P], diag_d[:, b, :],
                              start=True, stop=True)
                last.then_inc(pr_ready, 1)

            def state_transpose(c, n):
                pe.wait_ge(s_ready, c.index * NS + n + 1)
                for k in range(NT):
                    wait(pe, taken[k], c.index * NS + n)
                    transposes(tr_bank[k], [v[n % RING][:, b, k * P:(k + 1) * P] for b in range(KD)]) \
                        .then_inc(tr_ready, 1)

            def post_y(c, h):
                pe.wait_ge(y_ready, c.index + 1)
                wait(pe, o_free, c.index * POST_USES + h + HEAD)
                transposes(o_bank, [acc[c.par][:, k, b * P:(b + 1) * P]
                                    for b in (2 * h, 2 * h + 1) for k in range(NT)]).then_inc(o_ready, 1)

            def post_out(c):
                pe.wait_ge(o_free, c.index * POST_USES + 2 + HEAD)
                for k in range(NT):
                    for b in range(KD):
                        last = mm(o_bank[:, k * DM:(k + 1) * DM], yT[:, b, k * P:(k + 1) * P], w_out[:, b, :],
                                  start=(b == 0), stop=(b == KD - 1))
                last.then_inc(o_ready, 1)

            def post_norm(c):
                pe.wait_ge(xn2_ready, c.index * NT + NT)
                pe.wait_ge(o_free, c.index * POST_USES + 3 + HEAD)
                transposes(o_bank, [xn2[c.par][:, k, b * P:(b + 1) * P] for b in range(KM) for k in range(NT)]) \
                    .then_inc(o_ready, 1)

            def post_route(c):
                pe.wait_ge(o_free, c.index * POST_USES + 4 + HEAD)
                for k in range(NT):
                    for b in range(KM):
                        last = mm(o_bank[:, k * FFNS:(k + 1) * FFNS], xn2T[:, b, k * P:(k + 1) * P], w_rt[:, b, :],
                                  start=(b == 0), stop=(b == KM - 1))
                last.then_inc(o_ready, 1)

            def post_rank(c):
                pe.wait_ge(sel_ready, c.index + 1)
                for k in range(NT + 1):
                    for b in range(min(k + 1, NT)):
                        last = mm(o_bank[:, k * EXPERTS:(k + 1) * EXPERTS], (upper if b == k else ones)[:, :],
                                  sel[:, b, :], start=(b == 0), stop=(b == min(k, NT - 1)))
                last.then_inc(o_ready, 1)

            def gate_up(c, u, w, xT):
                bank = gu_bank[(c.par + u) % 2]
                pe.wait_ge(hg_ready, c.index * UNITS + u + HEAD)
                pe.wait_ge(up_ready, c.index * UNITS + u + HEAD)
                rows = HROWS[u]
                for g in range(2):
                    col = g * HID + u * P
                    for b in range(KM):
                        last = mm(bank[0:rows, g * TC:(g + 1) * TC], w[:, b, col:col + rows], xT[:, b, :],
                                  start=(b == 0), stop=(b == KM - 1))
                last.then_inc(gu_ready, 1)

            def down(c, w):
                pe.wait_ge(h_ready, c.index * UNITS + HB + 1 + HEAD)
                pe.wait_ge(mix_done, c.index + HEAD)
                for k in range(NT):
                    for m in range(HB):
                        rows = HROWS[m]
                        last = mm(dn_bank[:, k * DM:(k + 1) * DM],
                                  hid[0:rows, hid_slot(c, m), k * P:(k + 1) * P], w[0:rows, m, :],
                                  start=(m == 0), stop=(m == HB - 1))
                last.then_inc(dn_ready, 1)

            def tile_transpose(t):
                pe.wait_ge(xt_loaded[t.par], t.pair * 16 + 16)
                pe.wait_ge(o_free, CHUNKS * POST_USES + t.index + HEAD)
                transposes(o_bank, [xt[t.par][:, k, b * P:(b + 1) * P] for b in range(KM) for k in range(NT)]) \
                    .then_inc(o_ready, 1)

            def project(c, slot):
                if slot < 4:
                    proj_conv(c, slot // 2, slot % 2)
                if slot in (5, 6):
                    proj_dt(c, slot - 5)
                if slot == 8:
                    proj_bc(c)
                if slot in (9, 10):
                    proj_z(c, slot - 9)
                if slot in (13, 14):
                    proj_skip(c, slot - 13)

            class Body(Phases):
                eng = pe

                def start(self):
                    pe.sem_inc(dn_ready, 1 + HEAD)
                    pe.wait_ge(w_raw, 16 * RAW_LOADS)
                    for t in range(TAPS):
                        for b in range(KM):
                            for m in range(KD):
                                last = mm(banks[t * KM + b][:, :], raw_x[:, m, b * P:(b + 1) * P],
                                          raw_conv[:, m, t, :], start=(m == 0), stop=(m == KD - 1))
                            last.then_inc(comp_mm, 1)
                    pe.wait_ge(comp_done, TAPS * KM + 1)
                    pe.wait_ge(low_done, TAPS * KM + 1)
                    pe.wait_ge(pool_const, 11)
                    pe.wait_ge(dve_const, 1)
                    pe.wait_ge(w_early, 16 * EARLY_LOADS)
                    proj_norm(Chunk(0, 0))
                    for slot in range(NS):
                        project(Chunk(0, 0), slot)
                    proj_norm(Chunk(0, 1))

                def __call__(self, scan, post, proj, norm):
                    for slot in range(NS):
                        if slot == 0 and post:
                            state_transpose(post, NS - 1)
                        if slot > 0 and scan:
                            state_transpose(scan, slot - 1)
                        if post and slot in (1, 2):
                            post_y(post, slot - 1)
                        if post and slot == 4:
                            post_out(post)
                        if post and slot == 7:
                            post_norm(post)
                        if post and slot == 8:
                            post_route(post)
                        if post and slot == 10:
                            post_rank(post)
                        if proj:
                            project(proj, slot)
                        if norm and slot == NS - 1:
                            proj_norm(norm)
                        if post:
                            for u in units_of(slot):
                                gate_up(post, u, w_gu, xn2T)
                            if slot == DOWN_SLOT:
                                down(post, w_dn)

                def before_tiles(self):
                    tile_transpose(Chunk(0, 0))

                def tile(self, t, last):
                    c = counted(t)
                    pe.wait_ge(o_free, CHUNKS * POST_USES + t.index + 1 + HEAD)
                    pe.wait_ge(gu_loaded[t.par], t.pair * 16 + 16)
                    gate_up(c, 0, t_gu[t.par], xtT[t.par])
                    if not last:
                        tile_transpose(t.plus(1))
                    gate_up(c, 1, t_gu[t.par], xtT[t.par])
                    if not (t.fixed() and t.index == 0):
                        self.tile_down(t.plus(-1))
                    gate_up(c, 2, t_gu[t.par], xtT[t.par])
                    if last:
                        self.tile_down(t)

                def tile_down(self, t):
                    pe.wait_ge(dn_loaded[t.par], t.pair * 16 + 16)
                    down(counted(t), t_dn[t.par])

            run(Body())

        @block.scalar
        def _(act):
            af = nc.scalar.activation

            def decays(c, n):
                if n == 0:
                    act.wait_ge(dt_ready, c.index + 1)
                wait(act, s_ready, c.index * NS + n - RING + 1)
                for b in range(KD):
                    last = af(da[n % RING][:, b, :], dt[c.par][:, b, :], ACT.Exp, scale=neg_a[:, b, n:n + 1])
                last.then_inc(da_ready, 1)

            def add_eps(c, n):
                act.wait_ge(v_mul, c.index * NS + n + 1)
                af(v[n % RING][:, :, :], v[n % RING][:, :, :], ACT.Identity, bias=eps_col[:, 0:1]).then_inc(v_ready, 1)

            def aid_product(c, n):
                i = n - AIDED[0]
                act.wait_ge(tr_ready, c.index * NS * NT + NT * n + NT)
                wait(act, aid_added, c.index * len(AIDED) + i - 1)
                af(aid[i % 2][:, :], tr_bank[1][:, :], ACT.Copy, scale=c_tok[c.par][:, 1, n:n + 1]) \
                    .then_inc(taken[1], 1)
                act.wait_ge(taken[1], c.index * NS + n + 1)
                act.sem_inc(aid_ready, 1)

            def take_normed(c):
                act.wait_ge(pr_ready, c.index * PROJ_USES + 1)
                if c.fixed() and c.index == 0:
                    af(xnT[0][:, :, 0:HALO], halo_zero[:, :, :], ACT.Copy)
                else:
                    tail = xnT[0][:, :, TC:TC + HALO]
                    if c.par == 0:
                        act.wait_ge(mask_done, c.pair)
                        af(xnT[0][:, :, 0:HALO], tail, ACT.Copy, scale=mask[:, 0:1]).then_inc(halo_done, 1)
                    else:
                        af(xnT[0][:, :, 0:HALO], tail, ACT.Copy).then_inc(halo_done, 1)
                    act.wait_ge(halo_done, c.index)
                af(xnT[0][:, :, HALO:HALO + TC], pr_bank[0][:, :].rearrange("p (b t) -> p b t", b=KM), ACT.Copy) \
                    .then_inc(evac, 1)

            def project(c, slot):
                done = c.index * PROJ_USES
                if slot in (2, 4):
                    h = slot // 2 - 1
                    act.wait_ge(pr_ready, done + 2 + h)
                    for j in range(2):
                        b = 2 * h + j
                        last = af(uT[:, b, :], pr_bank[1 - h][:, j * TC:(j + 1) * TC], ACT.Identity,
                                  bias=vec[:, 0, b:b + 1])
                    last.then_inc(evac, 1)
                if slot == 7:
                    for h in range(2):
                        act.wait_ge(pr_ready, done + 4 + h)
                        for j in range(2):
                            b = 2 * h + j
                            last = af(dt[c.par][:, b, :], pr_bank[1 - h][:, j * TC:(j + 1) * TC], ACT.Sigmoid,
                                      bias=vec[:, 1, b:b + 1])
                        last.then_inc(evac, 1)
                if slot == 8:
                    act.wait_ge(pr_ready, done + 6)
                    wait(act, b_written, c.index * 16)
                    af(b_row[:, :], pr_bank[1][0:NS, 0:TC], ACT.Copy).then_inc(b_ready, 1)
                    af(c_tok[c.par][:, :, :], pr_bank[1][:, TC:TC + NT * NS].rearrange("p (k n) -> p k n", k=NT),
                       ACT.Copy).then_inc(evac, 1)
                if slot in (9, 10):
                    k = slot - 9
                    act.wait_ge(pr_ready, done + 7 + k)
                    wait(act, y_ready, c.index - 1)
                    af(zs[c.par][:, k, :], pr_bank[k][:, :], ACT.Tanh, scale=0.5).then_inc(zt_ready, 1)
                if slot in (14, 15):
                    k = slot - 14
                    act.wait_ge(pr_ready, done + 9 + k)
                    af(acc[c.par][:, k, :], pr_bank[k][:, :], ACT.Copy).then_inc(evac, 1)

            def finish(c, slot):
                if slot in (1, 2):
                    h = slot - 1
                    act.wait_ge(o_ready, c.index * POST_USES + h + 1)
                    af(yT[:, 2 * h:2 * h + 2, :], o_bank[:, :].rearrange("p (b t) -> p b t", b=2), ACT.Copy) \
                        .then_inc(o_free, 1)
                if slot == 7:
                    act.wait_ge(o_ready, c.index * POST_USES + 4)
                    af(xn2T[:, :, :], o_bank[:, :].rearrange("p (b t) -> p b t", b=KM), ACT.Copy).then_inc(o_free, 1)
                if slot == 10:
                    act.wait_ge(r_in_ready, c.index * 2 + 2)
                    af(r_exp[:, :, :], r_in[:, :, :], ACT.Exp).then_inc(r_exp_ready, 1)

            def gate(c, u):
                rows = HROWS[u]
                bank = gu_bank[(c.par + u) % 2]
                act.wait_ge(gu_ready, c.index * UNITS + u + 1)
                act.wait_ge(dn_ready, c.index + HEAD)
                af(hid[0:rows, hid_slot(c, u), :], bank[0:rows, 0:TC], ACT.Tanh, scale=0.5).then_inc(th_ready, 1)
                act.wait_ge(h_ready, c.index * UNITS + u + HEAD)
                af(up[0:rows, (c.par + u) % 2, :], bank[0:rows, TC:2 * TC], ACT.Copy).then_inc(up_ready, 1)

            class Body(Phases):
                eng = act

                def start(self):
                    act.sem_inc(up_ready, 1 + HEAD)
                    act.wait_ge(w_early, 16 * EARLY_LOADS)
                    af(a_exp[:, :, :], a_raw[:, :, :], ACT.Exp).then_inc(a_exp_done, 1)
                    for n in range(TAPS * KM):
                        act.wait_ge(comp_mm, n + 1)
                        af(w_conv[0][:, n // KM, n % KM, :], banks[n][:, :], ACT.Copy).then_inc(comp_done, 1)
                    af(w_z[0][:, :, :], raw_z, ACT.Copy).then_inc(comp_done, 1)
                    act.wait_ge(pool_const, 11)
                    act.wait_ge(dve_const, 3)
                    take_normed(Chunk(0, 0))
                    for slot in range(NS):
                        project(Chunk(0, 0), slot)
                    take_normed(Chunk(0, 1))
                    for n in range(DECAY_LEAD):
                        decays(Chunk(0, 0), n)
                        add_eps(Chunk(0, 0), n)

                def __call__(self, scan, post, proj, norm):
                    for slot in range(NS):
                        n = slot + DECAY_LEAD
                        ahead = (None, 0) if not scan else (scan, n) if n < NS else (proj, n - NS)
                        if ahead[0]:
                            decays(*ahead)
                            add_eps(*ahead)
                        if scan and slot - 1 in AIDED:
                            aid_product(scan, slot - 1)
                        if post:
                            finish(post, slot)
                        if proj:
                            project(proj, slot)
                        if post:
                            for u in units_of(slot):
                                gate(post, u)
                        if norm and slot == NS - 1:
                            take_normed(norm)

                def before_tiles(self):
                    self.turned(Chunk(0, 0))

                def turned(self, t):
                    act.wait_ge(o_ready, CHUNKS * POST_USES + t.index + 1)
                    af(xtT[t.par], o_bank[:, :].rearrange("p (b t) -> p b t", b=KM), ACT.Copy).then_inc(o_free, 1)

                def tile(self, t, last):
                    c = counted(t)
                    gate(c, 0)
                    if not last:
                        self.turned(t.plus(1))
                    gate(c, 1)
                    if not (t.fixed() and t.index == 0):
                        self.tile_out(t.plus(-1))
                    gate(c, 2)
                    if last:
                        self.tile_out(t)

                def tile_out(self, t):
                    act.wait_ge(dn_ready, counted(t).index + 2 + HEAD)
                    if not (t.fixed() and t.pair == 0):
                        act.wait_ge(sent[t.par], t.pair * NT * 16)
                    act.wait_ge(ids_ready, t.index + 1)
                    for k in range(NT):
                        last = af(yt[t.par][:, k, :], dn_bank[:, k * DM:(k + 1) * DM], ACT.Copy,
                                  scale=wts[t.par][:, k:k + 1])
                    last.then_inc(yt_ready, 1)
                    act.wait_ge(yt_ready, t.index + 1)
                    act.sem_inc(mix_done, 1)

            run(Body())

        @block.gpsimd
        def _(pool):
            def b_times_dtu(c, n):
                piece = n // NEAR
                if n == 0:
                    pool.wait_ge(dtu_ready, c.index + 1)
                if n % NEAR == 0:
                    pool.wait_ge(b_loaded[piece % 2], (c.index * 2 + piece // 2 + 1) * 16)
                wait(pool, tr_ready, c.index * NS * NT + NT * (n - RING + 1))
                wait(pool, carry_done, c.index * NS + n - RING + 1)
                row = b_all[piece % 2][:, n % NEAR:n % NEAR + 1, :].to_broadcast([P, KD, TC])
                nc.gpsimd.tensor_tensor(out=v[n % RING][:, :, :], in0=dtu[c.par][:, :, :], in1=row, op=ALU.mult) \
                    .then_inc(v_mul, 1)

            def aid_sum(c, n):
                i = n - AIDED[0]
                pool.wait_ge(aid_ready, c.index * len(AIDED) + i + 1)
                pool.wait_ge(taken[1], c.index * NS + n)
                wait(pool, aid_added, c.index * len(AIDED) + i)
                a = acc[c.par][:, 1, :]
                nc.gpsimd.tensor_tensor(out=a, in0=a, in1=aid[i % 2][:, :], op=ALU.add).then_inc(aid_added, 1)

            def rstd(out, var, ready, done, c):
                pool.wait_ge(ready, c.index + 1)
                nc.gpsimd.tensor_tensor(out=out[:, :], in0=var[:, :], in1=neg_half[:, :], op=ALU.pow) \
                    .then_inc(done, 1)

            def scatter(c, n):
                pool.wait_ge(dest_ready, c.index * 2 + n + 1)
                pool.sem_inc(pool_settled, 1)
                for k in range(NT):
                    m = n * NT + k
                    nc.gpsimd.indirect_dma_start(
                        out=xg[:, :], out_offset=bass.IndirectOffsetOnAxis(ap=dest[c.par][:, m:m + 1], axis=0),
                        in_=xn2[c.par][:, k, :], in_offset=None).then_inc(scat_done[c.par], 16)

            def hidden(c, u):
                rows = HROWS[u]
                pool.wait_ge(hg_ready, c.index * UNITS + u + 2 + HEAD)
                pool.wait_ge(up_ready, c.index * UNITS + u + 2 + HEAD)
                block_ = hid[0:rows, hid_slot(c, u), :]
                nc.gpsimd.tensor_tensor(out=block_, in0=block_, in1=up[0:rows, (c.par + u) % 2, :], op=ALU.mult) \
                    .then_inc(h_ready, 1)

            class Body(Phases):
                eng = pool

                def start(self):
                    pool.sem_inc(h_ready, 1 + HEAD)
                    nc.gpsimd.memset(ident[:, :], 0.0).then_inc(pool_const, 1)
                    pool.wait_ge(pool_const, 1)
                    nc.gpsimd.affine_select(out=ident[:, :], in_=ident[:, :], compare_op=ALU.not_equal, fill=1.0,
                                            base=0, pattern=[[-1, P]], channel_multiplier=1).then_inc(pool_const, 1)
                    nc.gpsimd.memset(eps_col[:, :], STATE_EPS).then_inc(pool_const, 1)
                    nc.gpsimd.memset(halo_zero[:, :, :], 0.0).then_inc(pool_const, 1)
                    nc.gpsimd.memset(mask[:, :], 0.0).then_inc(pool_const, 1)
                    nc.gpsimd.memset(zeros[:, :, :], 0.0).then_inc(pool_const, 1)
                    nc.gpsimd.memset(xn2[0][:, :, DM:ROW], 0.0)
                    nc.gpsimd.memset(xn2[1][:, :, DM:ROW], 0.0)
                    nc.gpsimd.memset(ones[:, :], 1.0).then_inc(pool_const, 1)
                    pool.wait_ge(pool_const, 7)
                    nc.gpsimd.affine_select(out=upper[:, :], in_=ones[:, :], compare_op=ALU.is_gt, fill=0.0,
                                            base=0, pattern=[[1, P]], channel_multiplier=-1).then_inc(pool_const, 1)
                    nc.gpsimd.iota(zeros[:, :, ID_COL:ID_COL + 1].bitcast(I32), pattern=[[P, NT]], base=TOK,
                                   channel_multiplier=1)
                    nc.gpsimd.iota(token_i[:, :], pattern=[[P, NT]], base=0, channel_multiplier=1)
                    nc.gpsimd.iota(step_i[:, :], pattern=[[1, TILES]], base=0, channel_multiplier=0) \
                        .then_inc(pool_const, 1)
                    nc.gpsimd.iota(iota_i[:, :], pattern=[[1, EXPERTS]], base=0, channel_multiplier=0) \
                        .then_inc(pool_const, 1)
                    nc.gpsimd.memset(neg_half[:, :], -0.5).then_inc(pool_const, 1)
                    pool.wait_ge(pool_const, 11)
                    for i in range(2):
                        pool.dma_start(xg[EXPERTS * CAP + i * P:EXPERTS * CAP + (i + 1) * P, :], zeros[:, i, :]) \
                            .then_inc(scat_done[i], 16)
                        pool.dma_start(out[TOK + i * P:TOK + (i + 1) * P, :], zeros[:, 0, 0:DM]) \
                            .then_inc(dump_zero, 16)
                    for n in range(2):
                        rstd(p_rstd, p_var, p_var_ready, p_rstd_ready, Chunk(0, n))
                    pool.wait_ge(dve_const, 4)
                    nc.gpsimd.partition_all_reduce(a_max[:, 1:2], a_max[:, 0:1], P, bass.bass_isa.ReduceOp.max) \
                        .then_inc(a_max_done, 1)
                    for n in range(MUL_LEAD):
                        b_times_dtu(Chunk(0, 0), n)

                def __call__(self, scan, post, proj, norm):
                    for slot in range(NS):
                        n = slot + MUL_LEAD
                        if scan and n < NS:
                            b_times_dtu(scan, n)
                        if scan and proj and n >= NS:
                            b_times_dtu(proj, n - NS)
                        if scan and slot - 1 in AIDED:
                            aid_sum(scan, slot - 1)
                        if post and slot == 5:
                            rstd(o_rstd, o_var, o_var_ready, o_rstd_ready, post)
                        if norm and slot == 2:
                            rstd(p_rstd, p_var, p_var_ready, p_rstd_ready, norm)
                        if post:
                            for u in units_of(slot):
                                hidden(post, u)
                        if post and slot == 12:
                            scatter(post, 0)
                        if post and slot == 15:
                            scatter(post, 1)

                def before_tiles(self):
                    for i in range(2):
                        pool.wait_ge(x1_stored[i], 16 * (CHUNKS // 2) + 16)
                    pool.wait_ge(dump_zero, 16 * NT)

                def tile(self, t, last):
                    hidden(counted(t), 0)
                    hidden(counted(t), 1)
                    if not (t.fixed() and t.index == 0):
                        self.send(t.plus(-1))
                    hidden(counted(t), 2)
                    if last:
                        self.send(t)

                def send(self, t):
                    pool.wait_ge(yt_ready, t.index + 1)
                    pool.wait_ge(ids_ready, t.index + 1)
                    if not (t.fixed() and t.index == 0):
                        last = t.plus(-1)
                        pool.wait_ge(sent[last.par], (last.pair + 1) * NT * 16)
                    pool.sem_inc(pool_settled, 1)
                    for k in range(NT):
                        nc.gpsimd.indirect_dma_start(
                            out=out[:, :], out_offset=bass.IndirectOffsetOnAxis(
                                ap=ids[t.par][:, k:k + 1], axis=0),
                            in_=yt[t.par][:, k, :], in_offset=None, compute_op=ALU.add).then_inc(sent[t.par], 16)

            run(Body())

        @block.vector
        def _(dve):
            vec_e = nc.vector

            def settle():
                dve.sem_inc(settled, 1)

            class Steps:

                def __init__(self, sem_, per, c):
                    self.sem, self.per, self.c, self.k = sem_, per, c, 0

                def did(self, ins):
                    self.k += 1
                    ins.then_inc(self.sem, 1)

                def sync(self):
                    dve.wait_ge(self.sem, self.c.index * self.per + self.k)

            def stats(c, src, st, mv, var, step, ready):
                for k in range(NT):
                    step.did(vec_e.bn_stats(st[:, k, :], src[:, k, :]))
                step.sync()
                settle()
                for k in range(NT):
                    step.did(vec_e.bn_aggr(mv[:, k, :], st[:, k, :]))
                step.sync()
                vec_e.tensor_scalar_add(var[:, :], mv[:, :, 1], LN_EPS).then_inc(ready, 1)

            def normed(dst, src, mv, rstd, ready):
                for k in range(NT):
                    vec_e.tensor_scalar(out=dst[:, k, 0:DM], in0=src[:, k, :], scalar1=mv[:, k, 0:1],
                                        scalar2=rstd[:, k:k + 1], op0=ALU.subtract, op1=ALU.mult).then_inc(ready, 1)

            def norm_stats(c):
                dve.wait_ge(x_loaded[c.par], c.pair * 16 + 16)
                stats(c, x_in[c.par], p_st, p_mv, p_var, Steps(norm_step, NORM_STEPS, c), p_var_ready)

            def norm_apply(c):
                dve.wait_ge(p_rstd_ready, c.index + 1)
                normed(x_in[c.par], x_in[c.par], p_mv, p_rstd, xn_ready)

            def low_normed(c):
                if c.fixed() and c.index == 0:
                    vec_e.tensor_copy(xnT[1][:, :, 0:HALO], halo_zero[:, :, :])
                else:
                    tail = xnT[1][:, :, TC:TC + HALO]
                    if c.par == 0:
                        dve.wait_ge(mask_done, c.pair)
                        vec_e.tensor_scalar(out=xnT[1][:, :, 0:HALO], in0=tail, scalar1=mask[:, 0:1], scalar2=None,
                                            op0=ALU.mult).then_inc(halo_low, 1)
                    else:
                        vec_e.tensor_copy(xnT[1][:, :, 0:HALO], tail).then_inc(halo_low, 1)
                    dve.wait_ge(halo_low, c.index)
                dve.wait_ge(evac, c.index * EVACS + 1)
                vec_e.tensor_tensor(out=xnT[1][:, :, HALO:HALO + TC],
                                    in0=pr_bank[0][:, :].rearrange("p (b t) -> p b t", b=KM),
                                    in1=xnT[0][:, :, HALO:HALO + TC], op=ALU.subtract).then_inc(xn_low, 1)

            def proj_dt(c):
                dve.wait_ge(evac, c.index * EVACS + 5)
                d = dt[c.par][:, :, :]
                vec_e.tensor_scalar(out=d, in0=d, scalar1=DT_MIN, scalar2=DT_MAX, op0=ALU.max, op1=ALU.min) \
                    .then_inc(dt_ready, 1)
                dve.wait_ge(dt_ready, c.index + 1)
                vec_e.tensor_tensor(out=dtu[c.par][:, :, :], in0=d, in1=uT[:, :, :], op=ALU.mult) \
                    .then_inc(dtu_ready, 1)

            def proj_gate(c, k):
                dve.wait_ge(zt_ready, c.index * NT + k + 1)
                g = zs[c.par][:, k, :]
                vec_e.scalar_tensor_tensor(out=g, in0=g, scalar=1.0, in1=pr_bank[k][:, :], op0=ALU.add,
                                           op1=ALU.mult).then_inc(zs_done, 1)

            def scans(c, n, flag):
                with dve.If(flag > 0):
                    dve.wait_ge(da_ready, c.index * NS + n + 1)
                    vec_e.tensor_scalar_max(da[n % RING][:, :, :], da[n % RING][:, :, :], CLIP_EXP).then_inc(clip_done, 1)
                    dve.wait_ge(clip_done, c.index * NS + n + 1)
                    settle()
                dve.wait_ge(da_ready, c.index * NS + n + 1)
                if n == 0:
                    wait(dve, carry_done, c.index * NS)
                dve.wait_ge(v_ready, c.index * NS + n + 1)
                for b in range(KD):
                    init = 0.0 if c.fixed() and c.index == 0 else carry[:, n, b:b + 1]
                    s = v[n % RING][:, b, :]
                    last = vec_e.tensor_tensor_scan(s, da[n % RING][:, b, :], s, init, ALU.mult, ALU.add)
                last.then_inc(s_ready, 1)

            def keep_last(c, n):
                dve.wait_ge(s_ready, c.index * NS + n + 1)
                src = v[n % RING][:, :, TC - 1]
                if c.par:
                    if n == 0:
                        dve.wait_ge(mask_done, c.pair + 1)
                    vec_e.tensor_scalar(out=carry[:, n, :], in0=src, scalar1=mask[:, 0:1], scalar2=None,
                                        op0=ALU.mult).then_inc(carry_done, 1)
                else:
                    vec_e.tensor_copy(carry[:, n, :], src).then_inc(carry_done, 1)

            def c_times_state(c, n):
                for k in range(NT):
                    if k == 1 and n in AIDED:
                        continue
                    if n == 0:
                        dve.wait_ge(evac, c.index * EVACS + 8)
                    dve.wait_ge(tr_ready, c.index * NS * NT + NT * n + k + 1)
                    if k == 1 and AIDED and n == AIDED[-1] + 1:
                        dve.wait_ge(aid_added, (c.index + 1) * len(AIDED))
                    if n > 0:
                        dve.wait_ge(taken[k], c.index * NS + n)
                    a = acc[c.par][:, k, :]
                    vec_e.scalar_tensor_tensor(out=a, in0=tr_bank[k][:, :], scalar=c_tok[c.par][:, k, n:n + 1],
                                               in1=a, op0=ALU.mult, op1=ALU.add).then_inc(taken[k], 1)

            def post_gate(c):
                for k in range(NT):
                    dve.wait_ge(taken[k], (c.index + 1) * NS)
                dve.wait_ge(zs_done, (c.index + 1) * NT)
                a = acc[c.par][:, :, :]
                vec_e.scalar_tensor_tensor(out=a, in0=a, scalar=0.5, in1=zs[c.par][:, :, :], op0=ALU.mult,
                                           op1=ALU.mult).then_inc(y_ready, 1)

            def finish(c, slot, step):
                if slot == 0:
                    post_gate(c)
                if slot == 5:
                    dve.wait_ge(o_ready, c.index * POST_USES + 3)
                    dve.wait_ge(res_loaded, c.index * 16 + 16)
                    dve.wait_ge(x1_stored[c.par], c.pair * 16 + 16)
                    r = x1[c.par][:, :, :].rearrange("p k d -> p (k d)")
                    step.did(vec_e.tensor_tensor(out=r, in0=o_bank[:, :], in1=x_res[:, :, :]
                                                 .rearrange("p k d -> p (k d)"), op=ALU.add))
                    step.sync()
                    dve.sem_inc(x1_ready, 1)
                    dve.sem_inc(o_free, 1)
                    stats(c, x1[c.par], o_st, o_mv, o_var, step, o_var_ready)
                if slot == 6:
                    dve.wait_ge(o_rstd_ready, c.index + 1)
                    dve.wait_ge(scat_done[c.par], c.pair * PICKS * NT * 16 + 16)
                    normed(xn2[c.par], x1[c.par], o_mv, o_rstd, xn2_ready)
                if slot == 9:
                    dve.wait_ge(o_ready, c.index * POST_USES + 5)
                    vec_e.tensor_copy(lg[:, :, :], o_bank[:, 0:NT * FFNS].rearrange("p (k e) -> p k e", k=NT)) \
                        .then_inc(o_free, 1)
                    dve.wait_ge(o_free, c.index * POST_USES + 5 + HEAD)
                    settle()
                    for k in range(NT):
                        step.did(vec_e.max(top[:, k, :], lg[:, k, 0:EXPERTS]))
                    step.sync()
                    vec_e.tensor_tensor(out=r_in[:, 0, :], in0=top[:, :, 1], in1=top[:, :, 0], op=ALU.subtract) \
                        .then_inc(r_in_ready, 1)
                    vec_e.tensor_scalar_mul(r_in[:, 1, :], lg[:, :, EXPERTS], -1.0).then_inc(r_in_ready, 1)
                    for k in range(NT):
                        step.did(vec_e.max_index(top_i[:, k, :], top[:, k, :], lg[:, k, 0:EXPERTS]))
                    step.sync()
                    step.did(vec_e.tensor_copy(top_f[:, :, :], top_i[:, :, 0:2]))
                    step.sync()
                    for k in range(NT):
                        for n in range(PICKS):
                            step.did(vec_e.tensor_scalar(out=hot[:, n, k, :], in0=iota_f[:, :],
                                                         scalar1=top_f[:, k, n:n + 1], scalar2=None,
                                                         op0=ALU.is_equal))
                    step.sync()
                    vec_e.tensor_tensor(out=sel[:, :, :], in0=hot[:, 0, :, :], in1=hot[:, 1, :, :], op=ALU.add) \
                        .then_inc(sel_ready, 1)
                if slot == 11:
                    dve.wait_ge(r_exp_ready, c.index + 1)
                    step.did(vec_e.tensor_scalar_add(r_den[:, :, :], r_exp[:, :, :], 1.0))
                    step.sync()
                    step.did(vec_e.reciprocal(r_w[:, :, :], r_den[:, :, :]))
                    step.sync()
                    step.did(vec_e.tensor_scalar_mul(r_w[:, :, :], r_w[:, :, :], 0.5))
                    step.sync()
                    step.did(vec_e.tensor_copy(w_sh[c.par][:, :], r_w[:, 1, :]))
                    vec_e.tensor_copy(xn2[c.par][:, :, W_COL], r_w[:, 0, :])
                    step.did(vec_e.tensor_tensor(out=w_second[c.par][:, :], in0=r_exp[:, 0, :],
                                                 in1=r_w[:, 0, :], op=ALU.mult))
                if slot == 11:
                    dve.wait_ge(o_ready, c.index * POST_USES + 6)
                    for k in range(NT):
                        last = vec_e.tensor_tensor(out=row_of[:, k, :], in0=o_bank[:, k * EXPERTS:(k + 1) * EXPERTS],
                                                   in1=base[:, :], op=ALU.add)
                        step.did(last)
                    step.sync()
                    vec_e.tensor_tensor(out=base[:, :], in0=o_bank[:, NT * EXPERTS:(NT + 1) * EXPERTS],
                                        in1=base[:, :], op=ALU.add).then_inc(o_free, 1)
                    for n in range(PICKS):
                        last = vec_e.tensor_tensor(out=picked[:, n, :, :], in0=hot[:, n, :, :], in1=row_of[:, :, :],
                                                   op=ALU.mult)
                    step.did(last)
                    step.sync()
                    step.did(vec_e.tensor_reduce(dest_f[:, :], picked[:, :, :, :]
                                                 .rearrange("p n k e -> p (n k) e"), AX.X, ALU.add))
                    step.sync()
                    vec_e.tensor_copy(xn2[c.par][:, :, ID_COL].bitcast(U32), token_f[:, :])
                    vec_e.tensor_copy(dest[c.par][:, :], dest_f[:, :]).then_inc(dest_ready, 1)
                if slot == 15:
                    dve.wait_ge(scat_done[c.par], c.pair * PICKS * NT * 16 + 16 + NT * 16)
                    vec_e.tensor_copy(xn2[c.par][:, :, W_COL], w_second[c.par][:, :]).then_inc(dest_ready, 1)
                    step.did(vec_e.tensor_scalar_add(token_f[:, :], token_f[:, :], float(TC)))
                    assert step.k == POST_STEPS, step.k

            def gated(c, u):
                rows = HROWS[u]
                dve.wait_ge(th_ready, c.index * UNITS + u + 1)
                dve.wait_ge(up_ready, c.index * UNITS + u + 2 + HEAD)
                h = hid[0:rows, hid_slot(c, u), :]
                vec_e.scalar_tensor_tensor(out=h, in0=h, scalar=1.0, in1=gu_bank[(c.par + u) % 2][0:rows, 0:TC],
                                           op0=ALU.add, op1=ALU.mult).then_inc(hg_ready, 1)

            def mix(c):
                dve.wait_ge(dn_ready, c.index + 2 + HEAD)
                for k in range(NT):
                    r = x1[c.par][:, k, :]
                    last = vec_e.scalar_tensor_tensor(out=r, in0=dn_bank[:, k * DM:(k + 1) * DM],
                                                      scalar=w_sh[c.par][:, k:k + 1], in1=r, op0=ALU.mult,
                                                      op1=ALU.add)
                last.then_inc(mix_done, 1)

            def tile_table():
                done = [0]

                def did(ins):
                    done[0] += 1
                    ins.then_inc(table_step, 1)
                    dve.wait_ge(table_step, done[0])

                full = [P, TILES, EXPERTS]
                did(vec_e.tensor_copy(tab_zero[:, :], base[:, :]))
                did(vec_e.tensor_tensor(out=n_tok[:, :], in0=base[:, :], in1=first_row[:, :], op=ALU.subtract))
                did(vec_e.tensor_scalar_mul(t_row[:, :], step_f[:, :], float(TILE)))
                did(vec_e.tensor_tensor(
                    out=n_gt[:, :, :], in0=n_tok[:, :].unsqueeze(2).to_broadcast([P, EXPERTS, TOK // TILE]),
                    in1=t_row[:, 0:TOK // TILE].unsqueeze(1).to_broadcast([P, EXPERTS, TOK // TILE]), op=ALU.is_gt))
                did(vec_e.tensor_reduce(n_tiles[:, :], n_gt[:, :, :], AX.X, ALU.add))
                did(vec_e.tensor_tensor_scan(n_incl[:, :], ones[:, 0:EXPERTS], n_tiles[:, :], 0.0, ALU.mult, ALU.add))
                did(vec_e.tensor_tensor(out=past[:, :, :], in0=n_incl[:, :].unsqueeze(1).to_broadcast(full),
                                        in1=step_f[:, :].unsqueeze(2).to_broadcast(full), op=ALU.is_le))
                did(vec_e.tensor_reduce(t_exp[:, :], past[:, :, :], AX.X, ALU.add))
                did(vec_e.tensor_tensor(out=past_t[:, :, :], in0=past[:, :, :],
                                        in1=n_tiles[:, :].unsqueeze(1).to_broadcast(full), op=ALU.mult))
                did(vec_e.tensor_reduce(t_used[:, :], past_t[:, :, :], AX.X, ALU.add))
                did(vec_e.tensor_tensor(out=t_row[:, :], in0=step_f[:, :], in1=t_used[:, :], op=ALU.subtract))
                did(vec_e.tensor_scalar_mul(t_row[:, :], t_row[:, :], float(TILE)))
                did(vec_e.tensor_scalar_mul(t_used[:, :], t_exp[:, :], float(CAP)))
                did(vec_e.tensor_tensor(out=t_row[:, :], in0=t_row[:, :], in1=t_used[:, :], op=ALU.add))
                did(vec_e.tensor_copy(tab[:, 0, :], t_exp[:, :]))
                did(vec_e.tensor_scalar_min(t_row[:, :], t_row[:, :], float(EXPERTS * CAP)))
                vec_e.tensor_copy(tab[:, 1, :], t_row[:, :]).then_inc(tab_ready, 1)

            class Body(Phases):
                eng = dve

                def start(self):
                    dve.sem_inc(hg_ready, 1 + HEAD)
                    dve.sem_inc(o_free, HEAD)
                    dve.sem_inc(mix_done, HEAD)
                    dve.wait_ge(w_early, 16 * EARLY_LOADS)
                    dve.wait_ge(pool_const, 11)
                    for b in range(KD):
                        last = vec_e.tensor_scalar(out=diag_d[:, b, :], in0=ident[:, :], scalar1=vec[:, 2, b:b + 1],
                                                   scalar2=None, op0=ALU.mult)
                    last.then_inc(dve_const, 1)
                    vec_e.tensor_copy(step_f[:, :], step_i[:, :])
                    vec_e.tensor_copy(token_f[:, :], token_i[:, :])
                    vec_e.tensor_copy(iota_f[:, :], iota_i[:, :]).then_inc(dve_const, 1)
                    dve.wait_ge(dve_const, 2)
                    vec_e.tensor_scalar_mul(first_row[:, :], iota_f[:, :], float(CAP))
                    vec_e.tensor_scalar_mul(base[:, :], iota_f[:, :], float(CAP))
                    dve.wait_ge(a_exp_done, 1)
                    vec_e.tensor_scalar_mul(neg_a[:, :, :], a_exp[:, :, :], -1.0).then_inc(dve_const, 1)
                    vec_e.reduce_max(a_max[:, 0:1], a_exp[:, :, :].rearrange("p b n -> p (b n)"), AX.X) \
                        .then_inc(dve_const, 1)
                    for n in range(2):
                        norm_stats(Chunk(0, n))
                        norm_apply(Chunk(0, n))
                    for n in range(TAPS * KM):
                        dve.wait_ge(comp_done, n + 1)
                        vec_e.tensor_tensor(out=w_conv[1][:, n // KM, n % KM, :], in0=banks[n][:, :],
                                            in1=w_conv[0][:, n // KM, n % KM, :], op=ALU.subtract) \
                            .then_inc(low_done, 1)
                    dve.wait_ge(comp_done, TAPS * KM + 1)
                    vec_e.tensor_tensor(out=w_z[1][:, :, :], in0=raw_z, in1=w_z[0][:, :, :], op=ALU.subtract) \
                        .then_inc(low_done, 1)
                    low_normed(Chunk(0, 0))
                    dve.wait_ge(a_max_done, 1)
                    vec_e.tensor_scalar(out=a_flag[:, :], in0=a_max[:, 1:2], scalar1=CLIP, scalar2=None,
                                        op0=ALU.is_gt).then_inc(dve_const, 1)
                    dve.wait_ge(dve_const, 5)
                    self.flag = dve.value_load(a_flag[0:1, 0:1], min_val=0, max_val=1)
                    proj_dt(Chunk(0, 0))
                    proj_gate(Chunk(0, 0), 0)
                    proj_gate(Chunk(0, 0), 1)

                def __call__(self, scan, post, proj, norm):
                    step = Steps(post_step, POST_STEPS, post) if post else None
                    for slot in range(NS):
                        if slot == 0 and scan and not scan.par:
                            vec_e.tensor_scalar(out=mask[:, :], in0=mask[:, :], scalar1=-1.0, scalar2=1.0,
                                                op0=ALU.mult, op1=ALU.add).then_inc(mask_done, 1)
                        if scan:
                            scans(scan, slot, self.flag)
                        if slot == 0 and proj:
                            low_normed(proj)
                        if slot == 0 and post:
                            c_times_state(post, NS - 1)
                        if slot > 0 and scan:
                            c_times_state(scan, slot - 1)
                        if scan:
                            keep_last(scan, slot)
                        if post:
                            finish(post, slot, step)
                        if proj and slot == 8:
                            proj_dt(proj)
                        if proj and slot in (12, 13):
                            proj_gate(proj, slot - 12)
                        if norm and slot == 2:
                            norm_stats(norm)
                        if norm and slot == 3:
                            norm_apply(norm)
                        if post:
                            for u in units_of(slot):
                                gated(post, u)
                            if slot == MIX_SLOT:
                                mix(post)

                def before_tiles(self):
                    tile_table()

                def tile(self, t, last):
                    dve.wait_ge(xt_loaded[t.par], t.pair * 16 + 16)
                    if not (t.fixed() and t.pair == 0):
                        dve.wait_ge(sent[t.par], t.pair * NT * 16)
                    vec_e.tensor_copy(ids[t.par][:, :], xt[t.par][:, :, ID_COL].bitcast(U32))
                    vec_e.tensor_copy(wts[t.par][:, :], xt[t.par][:, :, W_COL]).then_inc(ids_ready, 1)
                    for u in range(UNITS):
                        gated(counted(t), u)

            assert PER_SEQ == 4
            run(Body())


def kernel(**inputs):
    import numpy as np
    import concourse.bacc as bacc
    from concourse import mybir as _mybir
    from concourse.bass_utils import run_bass_kernel_spmd

    g = {k: np.asarray(v) for k, v in inputs.items()}
    cont = np.ascontiguousarray

    def rows(a):
        return cont(a.reshape(-1, P, a.shape[1]).transpose(1, 0, 2))

    def cols(a):
        return cont(np.moveaxis(a.reshape(-1, P, *a.shape[1:]), 0, 1))

    in_w = g["L0_attn_in_proj_w"]
    gu = np.concatenate([np.concatenate([g["L0_ffn_w_gate"], g["L0_ffn_w_up"]], axis=2),
                         np.concatenate([g["L0_ffn_sw_gate"], g["L0_ffn_sw_up"]], axis=1)[None]], axis=0)
    dn = np.concatenate([g["L0_ffn_w_down"], g["L0_ffn_sw_down"][None]], axis=0)
    dn = np.concatenate([dn, np.zeros((FFNS, HB * P - HID, DM), dn.dtype)], axis=1)
    arrays = {
        "x": cont(g["L0_attn_x"].reshape(TOK, DM)),
        "wx": rows(in_w[0:DI]),
        "wconv": cont(g["L0_attn_conv_w"].transpose(1, 2, 0).reshape(KD, P, TAPS, DI).transpose(1, 0, 2, 3)),
        "wz": rows(in_w[DI:2 * DI].T),
        "wdt": rows(g["L0_attn_dt_w"].T),
        "wbc": rows(np.concatenate([g["L0_attn_B_w"], g["L0_attn_C_w"]], axis=0).T),
        "wout": rows(g["L0_attn_out_w"].T),
        "conv_b": cols(g["L0_attn_conv_b"]),
        "dt_b": cols(g["L0_attn_dt_b"]),
        "d_skip": cols(g["L0_attn_D"]),
        "a_log": cols(g["L0_attn_A_log"]),
        "wgate": rows(np.concatenate([g["L0_ffn_gate_w"], g["L0_ffn_shared_gate_w"]], axis=0).T),
        "wgu": cont(gu.reshape(FFNS, KM, P, 2 * HID).transpose(0, 2, 1, 3)),
        "wd": cont(dn.reshape(FFNS, HB, P, DM).transpose(0, 2, 1, 3)),
    }
    nc = bacc.Bacc("TRN2", target_bir_lowering=False, num_devices=1)
    args = [nc.dram_tensor(f"in_{k}", a.shape, _mybir.dt.from_np(a.dtype), kind="ExternalInput").ap()
            for k, a in arrays.items()]
    out = nc.dram_tensor("out_0", (OUT_ROWS, DM), F32, kind="ExternalOutput").ap()
    build(nc, *args, out)
    r = run_bass_kernel_spmd(nc, [{f"in_{k}": a for k, a in arrays.items()}], core_ids=[0])
    return r.results[0]["out_0"][:TOK].reshape(BATCH, SEQ, DM)
```
